# Optimizing a Trainium2 kernel written in Bass

```python
import numpy as np
import jax
import jax.numpy as jnp

def _softmax(x, axis=-1):
    return jax.nn.softmax(x, axis=axis)

def _gelu(x):
    return jax.nn.gelu(x, approximate=True)

def _silu(x):
    return jax.nn.silu(x)

def _sigmoid(x):
    return jax.nn.sigmoid(x)

def _layernorm(x, axis=-1, eps=1e-05):
    m = jnp.mean(x, axis=axis, keepdims=True)
    v = jnp.var(x, axis=axis, keepdims=True)
    return (x - m) / jnp.sqrt(v + eps)

def _scatter_add(tgt, idx, src, axis=0):
    return tgt.at[idx].add(src)

def _segment_sum(src, seg, n):
    return jax.ops.segment_sum(src, seg, n)
kernel_name = 'mk_recurrent_d1_jaxref_r4_177763'

def setup_inputs(seed: int=0):
    np.random.seed(seed)
    _w = jnp.asarray

    def _L0_attn_setup():
        import jax, jax.numpy as jnp
        import numpy as np
        D_INNER = 512
        D_STATE = 16
        DT_RANK = 128
        BATCH = 2
        SEQLEN = 512
        key = jax.random.key(seed)
        ks = jax.random.split(key, 5)
        x = jax.random.normal(ks[0], (BATCH, SEQLEN, D_INNER), dtype=jnp.float32)
        x_proj_w = jax.random.normal(ks[1], (DT_RANK + 2 * D_STATE, D_INNER), dtype=jnp.float32) * (1.0 / np.sqrt(D_INNER))
        dt_proj_w = jax.random.normal(ks[2], (D_INNER, DT_RANK), dtype=jnp.float32) * (1.0 / np.sqrt(DT_RANK))
        dt_proj_b = jax.random.normal(ks[3], (D_INNER,), dtype=jnp.float32) * 0.1
        a_init = jnp.broadcast_to(jnp.arange(1, D_STATE + 1, dtype=jnp.float32)[None, :], (D_INNER, D_STATE))
        A_log = jnp.log(a_init)
        D_param = jnp.ones((D_INNER,), dtype=jnp.float32)
        return {'x': x, 'x_proj_w': x_proj_w, 'dt_proj_w': dt_proj_w, 'dt_proj_b': dt_proj_b, 'A_log': A_log, 'D_param': D_param}
    _L0_attn_in = _L0_attn_setup()

    def _L0_ffn_setup():
        import jax, jax.numpy as jnp
        import numpy as np
        N, S, D = (8, 512, 512)
        O = 512
        E = 8
        K = 2
        key = jax.random.key(seed)
        ks = jax.random.split(key, 5)
        scale_in = 1.0 / np.sqrt(D)
        x = jax.random.normal(ks[0], (N, S, D), dtype=jnp.float32)
        gate_w = jax.random.uniform(ks[1], (D, E), dtype=jnp.float32, minval=-scale_in, maxval=scale_in)
        gate_b = jax.random.uniform(ks[2], (E,), dtype=jnp.float32, minval=-scale_in, maxval=scale_in)
        expert_w = jax.random.uniform(ks[3], (E, D, O), dtype=jnp.float32, minval=-scale_in, maxval=scale_in)
        expert_b = jax.random.uniform(ks[4], (E, O), dtype=jnp.float32, minval=-scale_in, maxval=scale_in)
        return {'x': x, 'gate_w': gate_w, 'gate_b': gate_b, 'expert_w': expert_w, 'expert_b': expert_b}
    _L0_ffn_in = _L0_ffn_setup()
    _d = {'L0_attn_x': _L0_attn_in['x'], 'L0_attn_x_proj_w': _L0_attn_in['x_proj_w'], 'L0_attn_dt_proj_w': _L0_attn_in['dt_proj_w'], 'L0_attn_dt_proj_b': _L0_attn_in['dt_proj_b'], 'L0_attn_A_log': _L0_attn_in['A_log'], 'L0_attn_D_param': _L0_attn_in['D_param'], 'L0_ffn_gate_w': _L0_ffn_in['gate_w'], 'L0_ffn_gate_b': _L0_ffn_in['gate_b'], 'L0_ffn_expert_w': _L0_ffn_in['expert_w'], 'L0_ffn_expert_b': _L0_ffn_in['expert_b']}
    _x0 = _d['L0_attn_x']
    _d['L0_attn_x'] = jax.random.normal(jax.random.fold_in(jax.random.key(seed), 1), (16, 512, 512), dtype=_x0.dtype)
    del _x0
    return _d

def reference(L0_attn_x, L0_attn_x_proj_w, L0_attn_dt_proj_w, L0_attn_dt_proj_b, L0_attn_A_log, L0_attn_D_param, L0_ffn_gate_w, L0_ffn_gate_b, L0_ffn_expert_w, L0_ffn_expert_b):

    def _L0_attn_ref(x, x_proj_w, dt_proj_w, dt_proj_b, A_log, D_param):
        import jax, jax.numpy as jnp
        import numpy as np
        D_INNER = 512
        D_STATE = 16
        DT_RANK = 128
        BATCH = 2
        SEQLEN = 512
        dt_rank = dt_proj_w.shape[1]
        d_state = A_log.shape[1]
        x_dbl = jnp.einsum('bld,kd->blk', x, x_proj_w)
        delta_un = x_dbl[..., :dt_rank]
        Bm = x_dbl[..., dt_rank:dt_rank + d_state]
        Cm = x_dbl[..., dt_rank + d_state:]
        delta = jax.nn.softplus(jnp.einsum('blr,dr->bld', delta_un, dt_proj_w) + dt_proj_b)
        A = -jnp.exp(A_log)
        delta_a_exp = jnp.exp(jnp.einsum('bld,dn->bldn', delta, A))
        delta_b_x = jnp.einsum('bld,bln,bld->bldn', delta, Bm, x)
        dae_t = jnp.moveaxis(delta_a_exp, 1, 0)
        dbx_t = jnp.moveaxis(delta_b_x, 1, 0)
        C_t = jnp.moveaxis(Cm, 1, 0)

        def step(state, inp):
            dae, dbx, c = inp
            state = dae * state + dbx
            y = jnp.einsum('bdn,bn->bd', state, c)
            return (state, y)
        init = jnp.zeros((x.shape[0], x.shape[2], d_state), dtype=x.dtype)
        _, ys = jax.lax.scan(step, init, (dae_t, dbx_t, C_t))
        y = jnp.moveaxis(ys, 0, 1)
        return y + x * D_param

    def _L0_ffn_ref(x, gate_w, gate_b, expert_w, expert_b):
        import jax, jax.numpy as jnp
        import numpy as np
        N, S, D = (8, 512, 512)
        O = 512
        E = 8
        K = 2
        gate_logits = jnp.einsum('nsd,de->nse', x, gate_w) + gate_b
        _, top_idx = jax.lax.top_k(gate_logits, K)
        all_out = jax.nn.relu(jnp.einsum('nsd,edo->nseo', x, expert_w) + expert_b)
        sel = jnp.take_along_axis(all_out, top_idx[..., None], axis=2)
        return sel.mean(axis=2)
    x = L0_attn_x
    xn = _layernorm(x, axis=-1)
    s = _L0_attn_ref(xn, L0_attn_x_proj_w, L0_attn_dt_proj_w, L0_attn_dt_proj_b, L0_attn_A_log, L0_attn_D_param)
    g = _silu(_L0_ffn_ref(xn, L0_ffn_gate_w, L0_ffn_gate_b, L0_ffn_expert_w, L0_ffn_expert_b))
    x = x + s * g
    return x

_drawn_inputs = setup_inputs


def setup_inputs(seed=0):
    import zlib

    import numpy as np

    out = dict(_drawn_inputs(seed))
    spreads = {'L0_attn_D_param': (1.0, 0.2)}
    factors = {}
    for name, (base, spread) in spreads.items():
        noise = np.random.default_rng([zlib.crc32(name.encode()), seed]).standard_normal(out[name].shape)
        drawn = base * np.exp(spread * noise) if base else spread * noise
        out[name] = jnp.asarray(drawn.astype(out[name].dtype))
    for name, factor in factors.items():
        out[name] = (out[name] * factor).astype(out[name].dtype)
    return out
```

```python
from contextlib import ExitStack

import concourse.bass as bass
from concourse import mybir

ALU = mybir.AluOpType
ACT = mybir.ActivationFunctionType
F32 = mybir.dt.float32
U32 = mybir.dt.uint32

P = 128
LN_EPS = 1e-5
DA_BANKS = 3
P_SLOTS = 4
QUAD = 4

STEPS = {3: "Z1", 7: "NT0", 9: "NT1", 11: "NT2", 13: "NT3", 15: "NX1", 17: "NX2", 19: "Z2",
         21: "NG", 35: "Z3", 51: "NZ0"}
LEAD_STEPS = ["NT0", "NT1", "NT2", "NT3", "NX1", "NX2", "NG", "NZ0"]
ORDER = list(STEPS.values())


def build(nc, x, xw, dw, db, alog, dpar, gw, gb, ew, eb, out):
    B, T, D = x.shape
    R = dw.shape[0]
    N = alog.shape[2]
    E = gw.shape[1]
    DT, TT = D // P, T // P
    UNITS = DT * N
    NQ = N // QUAD
    GROUPS = E * TT
    ADDS = (E - 1) * TT
    GROUP_AT = {10 + (g * 3) // 2: g for g in range(GROUPS)}

    ctx = ExitStack()
    with ctx:
        def sb(name, shape, dt=F32):
            return ctx.enter_context(nc.sbuf_tensor(name, shape, dt))

        def psum(name, shape):
            return ctx.enter_context(nc.psum_tensor(name, shape, F32))

        def sem(name):
            return ctx.enter_context(nc.semaphore(name))

        bc_dram = nc.dram_tensor("bc_rows", (B, 2 * N * T), F32, kind="Internal").ap()

        scan_ps = psum("scan_ps", [P, DA_BANKS, T])
        y_ps = psum("y_ps", [P, 2, TT, P])
        exp_ps = psum("exp_ps", [P, 2, D])
        proj_ps = psum("proj_ps", [P, T])

        ident = sb("ident", [P, P])
        ones = sb("ones", [1, P])
        xw_sb = sb("xw_sb", [P, DT, R + 2 * N])
        dw_sb = sb("dw_sb", [P, D])
        db_sb = sb("db_sb", [P, DT])
        a_sb = sb("a_sb", [P, DT, N])
        dpar_sb = sb("dpar_sb", [P, DT])
        gw_sb = sb("gw_sb", [P, DT, E])
        gb_sb = sb("gb_sb", [1, E])
        eb_sb = sb("eb_sb", [E, D])
        pick = sb("pick", [E, E, P])
        iota = sb("iota", [P, E])
        w_sb = sb("w_sb", [P, 2, DT, D])
        xn = sb("xn", [P, TT, D])
        stats = sb("stats", [P, TT, 6])
        mv = sb("mv", [P, TT, 2])
        vpe = sb("vpe", [P, TT])
        rstd = sb("rstd", [P, TT])
        newt = sb("newt", [P, TT])
        xT = sb("xT", [P, 2, DT, T])
        dun = sb("dun", [P, 2, T])
        bc_row = sb("bc_row", [2 * N, T])
        b_sb = sb("b_sb", [P, N, T])
        c_sb = sb("c_sb", [P, N, T])
        delta = sb("delta", [P, 2, T])
        u_sb = sb("u_sb", [P, 2, T])
        pad = sb("pad", [P, 1])
        sp_a = sb("sp_a", [P, T])
        sp_r = sb("sp_r", [P, T])
        xD = sb("xD", [P, 2, T])
        dbx = sb("dbx", [P, 2, QUAD, T])
        p_sb = sb("p_sb", [P, P_SLOTS, T])
        logit = sb("logit", [P, TT, E])
        top = sb("top", [P, TT, 8])
        topi = sb("topi", [P, TT, 8], U32)
        topf = sb("topf", [P, TT, 8])
        hot = sb("hot", [P, 2, TT, E])
        half = sb("half", [P, 2, TT, E])
        acc = sb("acc", [P, TT, D])
        relu = sb("relu", [P, 2, D])
        sig = sb("sig", [P, 2, D])
        s_sb = sb("s_sb", [P, TT, D])
        xo = sb("xo", [P, 2, D])

        w_const = sem("w_const")
        x_in = sem("x_in")
        w_in = [sem("w_in0"), sem("w_in1")]
        b_in = [sem(f"b_in{q}") for q in range(NQ)]
        c_in = [sem(f"c_in{q}") for q in range(NQ)]
        xo_in = [sem("xo_in0"), sem("xo_in1")]
        bc_out = sem("bc_out")
        out_st = [sem("out_st0"), sem("out_st1")]
        const_p = sem("const_p")
        a_exp = sem("a_exp")
        a_ready = sem("a_ready")
        bn_part = sem("bn_part")
        bn_done = sem("bn_done")
        ln_act = sem("ln_act")
        xn_ready = sem("xn_ready")
        proj_done = sem("proj_done")
        proj_used = sem("proj_used")
        sp_step = sem("sp_step")
        sp_ready = sem("sp_ready")
        xd_ready = sem("xd_ready")
        delta_ready = sem("delta_ready")
        u_ready = sem("u_ready")
        gate_step = sem("gate_step")
        half_ready = sem("half_ready")
        da_ready = sem("da_ready")
        dbx_ready = sem("dbx_ready")
        scanned = sem("scanned")
        p_ready = sem("p_ready")
        p_used = sem("p_used")
        y_used = sem("y_used")
        e_done = sem("e_done")
        e_used = sem("e_used")
        e_added = sem("e_added")
        sig_step = sem("sig_step")
        sig_ready = sem("sig_ready")
        g_ready = sem("g_ready")
        sg_done = sem("sg_done")
        out_sum = sem("out_sum")

        def from_start(count):
            return max(count, 0) if isinstance(count, int) else count

        def is_last(b):
            return isinstance(b, int) and b == B - 1

        def is_first(b):
            return isinstance(b, int) and b == 0

        def step_no(b, name):
            if b is None:
                return LEAD_STEPS.index(name)
            order = [s for s in ORDER if s[0] != "N"] if is_last(b) else ORDER
            return b * len(ORDER) + (len(LEAD_STEPS) + order.index(name))

        def t_copied(b, dt):
            if isinstance(b, int) and b == 0:
                return step_no(None, f"NT{dt}") + 1
            return step_no(b - 1, f"NT{dt}") + 1

        block = ctx.enter_context(nc.Block())

        def over_batches(eng, body):
            body(0, 0)
            body(1, 1)
            with eng.Fori(1, B // 2 - 1) as i:
                body(i * 2, 0)
                body(i * 2 + 1, 1)
            body(B - 2, 0)
            body(B - 1, 1)

        @block.sync
        def _(sp):
            def load_x(b):
                sp.dma_start(xn[:], x[bass.ds(b, 1)].rearrange("a (t p) d -> p (a t) d", p=P)).then_inc(x_in, 16)

            def send_bc(b, no):
                sp.wait_ge(proj_used, no + 1)
                sp.dma_start(bc_dram[bass.ds(b, 1), :].rearrange("a (r t) -> (a r) t", t=T),
                             bc_row[:]).then_inc(bc_out, 16)

            def load_bc(b, q, which):
                dst, s, base = (b_sb, b_in, 0) if which == "b" else (c_sb, c_in, N * T)
                src = bc_dram[bass.ds(b, 1), base + q * QUAD * T:base + (q + 1) * QUAD * T]
                src = src.rearrange("a f -> (a f)").partition_broadcast(P)
                sp.dma_start(dst[:, q * QUAD:(q + 1) * QUAD, :].rearrange("p n t -> p (n t)"),
                             src).then_inc(s[q], 16)

            def load_w(b, e):
                sp.dma_start(w_sb[:, e % 2], ew[e].rearrange("(c k) o -> k c o", k=P)).then_inc(w_in[e % 2], 16)

            load_x(0)
            for dst, src in ((xw_sb[:], xw.rearrange("(c k) r -> k c r", k=P)), (dw_sb[:], dw),
                             (db_sb[:], db), (a_sb[:], alog), (dpar_sb[:], dpar),
                             (gw_sb[:], gw.rearrange("(c k) e -> k c e", k=P)), (gb_sb[:], gb), (eb_sb[:], eb)):
                sp.dma_start(dst, src).then_inc(w_const, 16)
            load_w(0, 0)
            load_w(0, 1)
            sp.wait_ge(proj_done, step_no(None, "NT3") + 1)
            load_x(1)
            send_bc(0, step_no(None, "NX2"))
            sp.wait_ge(bc_out, 16)
            for q in range(NQ):
                load_bc(0, q, "b")
                load_bc(0, q, "c")

            def load_xo(b, tt):
                sp.wait_ge(out_st[tt % 2], (b * 2 + tt // 2) * 16)
                sp.dma_start(xo[:, tt % 2], x[bass.ds(b, 1), tt * P:(tt + 1) * P, :].rearrange("a p d -> (a p) d")
                             ).then_inc(xo_in[tt % 2], 16)

            def store(b, tt):
                sp.wait_ge(out_sum, b * TT + tt + 1)
                sp.dma_start(out[bass.ds(b, 1), tt * P:(tt + 1) * P, :].rearrange("a p d -> (a p) d"),
                             xo[:, tt % 2]).then_inc(out_st[tt % 2], 16)

            def batch(b, par):
                if not is_first(b):
                    for tt in range(2):
                        load_xo(b - 1, tt)
                    for tt in range(2):
                        store(b - 1, tt)
                        load_xo(b - 1, tt + 2)
                for e in range(2, E):
                    sp.wait_ge(e_done, b * GROUPS + (e - 1) * TT)
                    load_w(b, e)
                    if e == 2 and not is_first(b):
                        for tt in range(2, TT):
                            store(b - 1, tt)
                    if e == 4 and not is_last(b):
                        if not (isinstance(b, int) and b == B - 2):
                            sp.wait_ge(proj_done, step_no(b, "NT3") + 1)
                            load_x(b + 2)
                        send_bc(b + 1, step_no(b, "NX2"))
                if not is_last(b):
                    for e in range(2):
                        sp.wait_ge(e_done, (b + 1) * GROUPS - (1 - e) * TT)
                        load_w(b, e)
                    sp.wait_ge(bc_out, (b + 2) * 16)
                    for q in range(NQ):
                        sp.wait_ge(dbx_ready, b * DT * NQ + (DT - 1) * NQ + q + 1)
                        load_bc(b + 1, q, "b")
                        sp.wait_ge(p_ready, b * UNITS + (DT - 1) * N + (q + 1) * QUAD)
                        load_bc(b + 1, q, "c")

            over_batches(sp, batch)
            for tt in range(2):
                load_xo(B - 1, tt)
            for tt in range(2):
                store(B - 1, tt)
                load_xo(B - 1, tt + 2)
            for tt in range(2, TT):
                store(B - 1, tt)
            for tt in range(2):
                sp.wait_ge(out_st[tt], B * 2 * 16)

        @block.gpsimd
        def _(pool):
            nc.gpsimd.memset(ones[:], 1.0).then_inc(const_p, 1)
            nc.gpsimd.memset(ident[:], 0.0).then_inc(const_p, 1)
            nc.gpsimd.memset(pick[:], 0.0).then_inc(const_p, 1)
            for e in range(E):
                nc.gpsimd.memset(iota[:, e:e + 1], float(e)).then_inc(const_p, 1)
            pool.wait_ge(const_p, 3 + E)
            nc.gpsimd.affine_select(out=ident[:], in_=ident[:], compare_op=ALU.not_equal, fill=1.0,
                                    base=0, pattern=[[-1, P]], channel_multiplier=1).then_inc(const_p, 1)
            nc.gpsimd.affine_select(out=pick[:], in_=pick[:], compare_op=ALU.not_equal, fill=1.0,
                                    base=0, pattern=[[-1, E], [0, P]], channel_multiplier=1).then_inc(const_p, 1)

            def dbx_quad(b, j):
                dt, q = j // NQ, j % NQ
                if q == 0:
                    pool.wait_ge(u_ready, b * DT + dt + 1)
                if dt == 0:
                    pool.wait_ge(b_in[q], (b + 1) * 16)
                pool.wait_ge(scanned, from_start((b * DT * NQ + j - 1) * QUAD))
                nc.gpsimd.tensor_tensor(dbx[:, j % 2], b_sb[:, q * QUAD:(q + 1) * QUAD, :],
                                        u_sb[:, dt % 2, :].unsqueeze(1).to_broadcast([P, QUAD, T]),
                                        ALU.mult).then_inc(dbx_ready, 1)

            def gate_value(b, tt):
                if tt % 2 == 0:
                    pool.wait_ge(sig_ready, b * 2 + tt // 2 + 1)
                nc.gpsimd.tensor_tensor(acc[:, tt], acc[:, tt], sig[:, tt % 2], ALU.mult).then_inc(g_ready, 1)

            def add_x(b, tt):
                pool.wait_ge(sg_done, b * TT + tt + 1)
                pool.wait_ge(xo_in[tt % 2], (b * 2 + tt // 2 + 1) * 16)
                nc.gpsimd.tensor_tensor(xo[:, tt % 2], xo[:, tt % 2], s_sb[:, tt], ALU.add).then_inc(out_sum, 1)

            def batch(b, par):
                for j in range(DT * NQ):
                    dbx_quad(b, j)
                    if not is_first(b):
                        if j == 1:
                            gate_value(b - 1, 0)
                            gate_value(b - 1, 1)
                        if j == 2:
                            gate_value(b - 1, 2)
                            gate_value(b - 1, 3)
                        if j in (3, 4):
                            add_x(b - 1, 2 * (j - 3))
                            add_x(b - 1, 2 * (j - 3) + 1)

            over_batches(pool, batch)
            for tt in range(TT):
                gate_value(B - 1, tt)
            for tt in range(TT):
                add_x(B - 1, tt)

        @block.scalar
        def _(act):
            def ln_root(b):
                act.wait_ge(bn_done, b * 8 + 3)
                nc.scalar.activation(rstd[:], vpe[:], ACT.Ln).then_inc(ln_act, 1)
                act.wait_ge(ln_act, b * 2 + 1)
                nc.scalar.activation(rstd[:], rstd[:], ACT.Exp, scale=-0.5).then_inc(ln_act, 1)

            def copy_t(b, par, dt, no):
                act.wait_ge(proj_done, no + 1)
                if dt == 0:
                    act.wait_ge(e_done, from_start((b - 1) * GROUPS))
                    act.wait_ge(u_ready, from_start((b - 1) * DT))
                nc.scalar.activation(xT[:, par, dt, :], proj_ps[:], ACT.Copy).then_inc(proj_used, 1)

            def copy_dun(b, par, no):
                act.wait_ge(proj_done, no + 1)
                nc.scalar.activation(dun[:, par, :], proj_ps[:], ACT.Copy).then_inc(proj_used, 1)

            def copy_bc(b, no):
                act.wait_ge(proj_done, no + 1)
                act.wait_ge(bc_out, b * 16)
                nc.scalar.activation(bc_row[:], proj_ps[0:2 * N, :], ACT.Copy).then_inc(proj_used, 1)

            def softplus(b, par, dt, no):
                k = b * DT + dt
                act.wait_ge(proj_done, no + 1)
                act.wait_ge(delta_ready, k)
                bias = db_sb[:, dt:dt + 1]
                nc.scalar.activation(sp_a[:], proj_ps[:], ACT.Abs, bias=bias).then_inc(sp_step, 1)
                nc.scalar.activation(sp_r[:], proj_ps[:], ACT.Relu, bias=bias).then_inc(proj_used, 1)
                act.wait_ge(sp_step, k * 2 + 1)
                nc.scalar.activation(sp_a[:], sp_a[:], ACT.Exp, scale=-1.0).then_inc(sp_step, 1)
                act.wait_ge(proj_used, t_copied(b, dt))
                act.wait_ge(p_used, from_start((k - 2) * N + 1))
                nc.scalar.activation(xD[:, dt % 2, :], xT[:, par, dt, :], ACT.Copy,
                                     scale=dpar_sb[:, dt:dt + 1]).then_inc(xd_ready, 1)
                act.wait_ge(sp_step, k * 2 + 2)
                nc.scalar.activation(sp_a[:], sp_a[:], ACT.Ln, bias=1.0).then_inc(sp_ready, 1)

            def da_unit(b, par, j):
                dt, n = j // N, j % N
                u = b * UNITS + j
                if n == 0:
                    act.wait_ge(delta_ready, b * DT + dt + 1)
                back = DA_BANKS if j >= DA_BANKS else (1 if j == 0 else DA_BANKS + 1)
                act.wait_ge(p_ready, from_start(u - back + 1))
                nc.scalar.activation(scan_ps[:, j % DA_BANKS, :], delta[:, dt % 2, :], ACT.Exp,
                                     scale=a_sb[:, dt, n:n + 1]).then_inc(da_ready, 1)

            def copy_y(b, dt):
                k = b * DT + dt
                act.wait_ge(p_used, (k + 1) * N)
                act.wait_ge(out_sum, b * TT)
                nc.scalar.activation(s_sb[:, :, dt * P:(dt + 1) * P], y_ps[:, dt % 2], ACT.Copy).then_inc(y_used, 1)

            def expert_relu(b, par, g):
                e, tt = g // TT, g % TT
                G = b * GROUPS + g
                act.wait_ge(e_done, G + 1)
                if g == 0:
                    act.wait_ge(half_ready, b + 1)
                if e == 0:
                    act.wait_ge(sg_done, from_start((b - 1) * TT + tt + 1))
                    dst = acc[:, tt]
                else:
                    a = b * ADDS + g - TT
                    act.wait_ge(e_added, from_start(a - 1))
                    dst = relu[:, g % 2]
                nc.scalar.activation(dst, exp_ps[:, g % 2], ACT.Relu,
                                     scale=half[:, par, tt, e:e + 1]).then_inc(e_used, 1)

            def sigmoid(b, pair, part):
                c = (b * 2 + pair) * 2
                src = acc[:, 2 * pair:2 * pair + 2]
                if part == 0:
                    act.wait_ge(e_added, (b + 1) * ADDS)
                    act.wait_ge(g_ready, b * TT + 2 * pair)
                    nc.scalar.activation(sig[:], src, ACT.Exp, scale=-1.0).then_inc(sig_step, 1)
                if part == 1:
                    act.wait_ge(sig_step, c + 1)
                    nc.scalar.activation(sig[:], sig[:], ACT.Ln, bias=1.0).then_inc(sig_step, 1)
                if part == 2:
                    act.wait_ge(sig_step, c + 2)
                    nc.scalar.activation(sig[:], sig[:], ACT.Exp, scale=-1.0).then_inc(sig_ready, 1)

            ln_root(0)
            act.wait_ge(w_const, 8 * 16)
            nc.scalar.activation(a_sb[:], a_sb[:], ACT.Exp).then_inc(a_exp, 1)
            for dt in range(DT):
                copy_t(0, 0, dt, step_no(None, f"NT{dt}"))
            copy_dun(0, 0, step_no(None, "NX1"))
            copy_bc(0, step_no(None, "NX2"))
            softplus(0, 0, 0, step_no(None, "NZ0"))
            act.wait_ge(a_ready, 1)

            def batch(b, par):
                nxt = not is_last(b)
                for j in range(UNITS):
                    if j == 4 and nxt:
                        ln_root(b + 1)
                    name = STEPS.get(j - 3)
                    if name and (nxt or name[0] != "N"):
                        no = step_no(b, name)
                        if name[:2] == "NT":
                            copy_t(b + 1, 1 - par, int(name[2]), no)
                        elif name == "NX1":
                            copy_dun(b + 1, 1 - par, no)
                        elif name == "NX2":
                            copy_bc(b + 1, no)
                        elif name == "NZ0":
                            softplus(b + 1, 1 - par, 0, no)
                        elif name[0] == "Z":
                            softplus(b, par, int(name[1]), no)
                    if j - 4 in GROUP_AT:
                        expert_relu(b, par, GROUP_AT[j - 4])
                    if j % N == 4 and (j >= N or not is_first(b)):
                        copy_y(b, j // N - 1) if j >= N else copy_y(b - 1, DT - 1)
                    if not is_first(b) and 5 <= j < 11:
                        sigmoid(b - 1, (j - 5) // 3, (j - 5) % 3)
                    da_unit(b, par, j)

            over_batches(act, batch)
            copy_y(B - 1, DT - 1)
            for pair in range(2):
                for part in range(3):
                    sigmoid(B - 1, pair, part)

        @block.vector
        def _(dve):
            def ln_stats(b, tt):
                dve.wait_ge(x_in, (b + 1) * 16)
                nc.vector.bn_stats(stats[:, tt, :], xn[:, tt, :]).then_inc(bn_done if tt == TT - 1 else bn_part, 1)

            def ln_var(b):
                dve.wait_ge(bn_part, (b + 1) * (TT - 1))
                dve.wait_ge(bn_done, b * 8 + 1)
                nc.vector.memset(pad[:], 0.0)
                for tt in range(TT):
                    last = nc.vector.bn_aggr(mv[:, tt, :], stats[:, tt, :])
                last.then_inc(bn_done, 1)
                dve.wait_ge(bn_done, b * 8 + 2)
                nc.vector.tensor_scalar(vpe[:], mv[:, :, 1], LN_EPS, None, ALU.add).then_inc(bn_done, 1)

            def ln_newton(b):
                dve.wait_ge(ln_act, b * 2 + 2)
                c = b * 8 + 3
                nc.vector.tensor_tensor(newt[:], rstd[:], rstd[:], ALU.mult).then_inc(bn_done, 1)
                dve.wait_ge(bn_done, c + 1)
                nc.vector.tensor_tensor(newt[:], newt[:], vpe[:], ALU.mult).then_inc(bn_done, 1)
                dve.wait_ge(bn_done, c + 2)
                nc.vector.tensor_scalar(newt[:], newt[:], -0.5, 1.5, ALU.mult, ALU.add).then_inc(bn_done, 1)
                dve.wait_ge(bn_done, c + 3)
                nc.vector.tensor_tensor(rstd[:], rstd[:], newt[:], ALU.mult).then_inc(bn_done, 1)
                dve.wait_ge(bn_done, c + 4)

            def ln_apply(b, tt):
                inst = nc.vector.tensor_scalar(xn[:, tt, :], xn[:, tt, :], mv[:, tt, 0:1], rstd[:, tt:tt + 1],
                                               ALU.subtract, ALU.mult)
                if tt == TT - 1:
                    inst.then_inc(bn_done, 1)
                else:
                    inst.then_inc(xn_ready, 1)

            def delta_u(b, par, dt):
                k = b * DT + dt
                dve.wait_ge(sp_ready, k + 1)
                dve.wait_ge(proj_used, t_copied(b, dt))
                dve.wait_ge(da_ready, from_start((k - 1) * N))
                nc.vector.tensor_tensor(delta[:, dt % 2, :], sp_a[:], sp_r[:], ALU.add).then_inc(delta_ready, 1)
                dve.wait_ge(delta_ready, k + 1)
                dve.wait_ge(dbx_ready, from_start((k - 1) * NQ))
                nc.vector.tensor_tensor(u_sb[:, dt % 2, :], delta[:, dt % 2, :], xT[:, par, dt, :],
                                        ALU.mult).then_inc(u_ready, 1)

            GATE_CHAIN = 4

            def gate(b, par, no):
                dve.wait_ge(proj_done, no + 1)
                nc.vector.tensor_copy(logit[:], proj_ps[:, 0:TT * E].rearrange("p (t e) -> p t e", e=E)
                                      ).then_inc(proj_used, 1)
                dve.wait_ge(proj_used, no + 1)
                nc.vector.memset(pad[:], 0.0)
                c = b * GATE_CHAIN
                for tt in range(TT):
                    last = nc.vector.max(top[:, tt, :], logit[:, tt, :])
                last.then_inc(gate_step, 1)
                dve.wait_ge(gate_step, c + 1)
                nc.vector.memset(pad[:], 0.0)
                for tt in range(TT):
                    last = nc.vector.max_index(topi[:, tt, :], top[:, tt, :], logit[:, tt, :])
                last.then_inc(gate_step, 1)
                dve.wait_ge(gate_step, c + 2)
                nc.vector.tensor_copy(topf[:], topi[:]).then_inc(gate_step, 1)
                dve.wait_ge(gate_step, c + 3)
                for tt in range(TT):
                    for s in range(2):
                        last = nc.vector.tensor_scalar(hot[:, s, tt, :], iota[:], topf[:, tt, s:s + 1], 0.5,
                                                       ALU.is_equal, ALU.mult)
                last.then_inc(gate_step, 1)
                dve.wait_ge(gate_step, c + 4)
                dve.wait_ge(e_used, from_start((b - 1) * GROUPS))
                nc.vector.tensor_tensor(half[:, par], hot[:, 0], hot[:, 1], ALU.add).then_inc(half_ready, 1)

            def scan(b, j):
                u = b * UNITS + j
                dve.wait_ge(da_ready, u + 1)
                if j % QUAD == 0:
                    dve.wait_ge(dbx_ready, b * DT * NQ + j // QUAD + 1)
                bank = scan_ps[:, j % DA_BANKS, :]
                nc.vector.tensor_tensor_scan(bank, bank, dbx[:, (j // QUAD) % 2, j % QUAD, :], 0.0,
                                             ALU.mult, ALU.add).then_inc(scanned, 1)

            def times_c(b, j):
                dt, n = j // N, j % N
                u = b * UNITS + j
                dve.wait_ge(scanned, u + 1)
                if dt == 0 and n % QUAD == 0:
                    dve.wait_ge(c_in[n // QUAD], (b + 1) * 16)
                dve.wait_ge(p_used, from_start(u - P_SLOTS + 1))
                nc.vector.tensor_tensor(p_sb[:, j % P_SLOTS, :], scan_ps[:, j % DA_BANKS, :], c_sb[:, n, :],
                                        ALU.mult).then_inc(p_ready, 1)

            def expert_add(b, g):
                tt = g % TT
                a = b * ADDS + g - TT
                dve.wait_ge(e_used, b * GROUPS + g + 1)
                dve.wait_ge(e_added, from_start(a - TT + 1))
                nc.vector.tensor_tensor(acc[:, tt], acc[:, tt], relu[:, g % 2], ALU.add).then_inc(e_added, 1)

            def times_g(b, tt):
                dve.wait_ge(y_used, (b + 1) * DT)
                dve.wait_ge(g_ready, b * TT + tt + 1)
                nc.vector.tensor_tensor(s_sb[:, tt], s_sb[:, tt], acc[:, tt], ALU.mult).then_inc(sg_done, 1)

            TIMES_G_AT = (9, 10, 12, 13)

            for tt in range(TT):
                ln_stats(0, tt)
            ln_var(0)
            ln_newton(0)
            for tt in range(TT):
                ln_apply(0, tt)
            dve.wait_ge(a_exp, 1)
            nc.vector.tensor_scalar(a_sb[:], a_sb[:], -1.0, None, ALU.mult).then_inc(a_ready, 1)
            dve.wait_ge(const_p, 5 + E)
            gate(0, 0, step_no(None, "NG"))
            delta_u(0, 0, 0)

            def batch(b, par):
                nxt = not is_last(b)
                for j in range(UNITS):
                    scan(b, j)
                    if nxt:
                        if j < 2:
                            ln_stats(b + 1, 2 * j)
                            ln_stats(b + 1, 2 * j + 1)
                        if j == 2:
                            ln_var(b + 1)
                        if j == 4:
                            ln_newton(b + 1)
                        if j in (5, 6):
                            ln_apply(b + 1, 2 * (j - 5))
                            ln_apply(b + 1, 2 * (j - 5) + 1)
                    name = STEPS.get(j - 2)
                    if name == "NG" and nxt:
                        gate(b + 1, 1 - par, step_no(b, name))
                    name = STEPS.get(j - 5)
                    if name and name[0] == "Z":
                        delta_u(b, par, int(name[1]))
                    if name == "NZ0" and nxt:
                        delta_u(b + 1, 1 - par, 0)
                    if j - 5 in GROUP_AT and GROUP_AT[j - 5] >= TT:
                        expert_add(b, GROUP_AT[j - 5])
                    if not is_first(b) and j in TIMES_G_AT:
                        times_g(b - 1, TIMES_G_AT.index(j))
                    if j >= 1:
                        times_c(b, j - 1)
                times_c(b, UNITS - 1)

            over_batches(dve, batch)
            for tt in range(TT):
                times_g(B - 1, tt)

        @block.tensor
        def _(pe):
            def bank_free(no):
                pe.wait_ge(proj_used, no)

            def turn_x(b, dt, no):
                bank_free(no)
                if dt == 0:
                    pe.wait_ge(bn_done, (b + 1) * 8)
                    pe.wait_ge(xn_ready, (b + 1) * (TT - 1))
                for tt in range(TT):
                    last = nc.tensor.matmul(proj_ps[:, tt * P:(tt + 1) * P], xn[:, tt, dt * P:(dt + 1) * P],
                                            ident[:], start=True, stop=True, is_transpose=True)
                last.then_inc(proj_done, 1)

            def x_proj(par, lo, hi, no):
                bank_free(no)
                for c in range(DT):
                    last = nc.tensor.matmul(proj_ps[0:hi - lo, :], xw_sb[:, c, lo:hi], xT[:, par, c, :],
                                            start=(c == 0), stop=(c == DT - 1))
                last.then_inc(proj_done, 1)

            def dt_proj(par, dt, no):
                bank_free(no)
                nc.tensor.matmul(proj_ps[:], dw_sb[:, dt * P:(dt + 1) * P], dun[:, par, :],
                                 start=True, stop=True).then_inc(proj_done, 1)

            def gate(par, no):
                bank_free(no)
                for tt in range(TT):
                    dst = proj_ps[:, tt * E:(tt + 1) * E]
                    for c in range(DT):
                        nc.tensor.matmul(dst, xT[:, par, c, tt * P:(tt + 1) * P], gw_sb[:, c, :],
                                         start=(c == 0), stop=False)
                    last = nc.tensor.matmul(dst, ones[:], gb_sb[:], start=False, stop=True)
                last.then_inc(proj_done, 1)

            def expert(b, par, g):
                e, tt = g // TT, g % TT
                if tt == 0:
                    pe.wait_ge(w_in[e % 2], (b * (E // 2) + e // 2 + 1) * 16)
                pe.wait_ge(e_used, from_start(b * GROUPS + g - 1))
                dst = exp_ps[:, g % 2]
                for c in range(DT):
                    nc.tensor.matmul(dst, xT[:, par, c, tt * P:(tt + 1) * P], w_sb[:, e % 2, c, :],
                                     start=(c == 0), stop=False)
                nc.tensor.matmul(dst, pick[:, e, :], eb_sb[:], start=False, stop=True).then_inc(e_done, 1)

            def add_y(b, j):
                dt, n = j // N, j % N
                k = b * DT + dt
                y = y_ps[:, dt % 2]
                if n == 0:
                    pe.wait_ge(y_used, from_start(k - 1))
                    pe.wait_ge(xd_ready, k + 1)
                    for tt in range(TT):
                        nc.tensor.matmul(y[:, tt, :], xD[:, dt % 2, tt * P:(tt + 1) * P], ident[:],
                                         start=(tt == 0), stop=False, is_transpose=True, skip_group_check=True)
                pe.wait_ge(p_ready, b * UNITS + j + 1)
                for tt in range(TT):
                    last = nc.tensor.matmul(y[:, tt, :], p_sb[:, j % P_SLOTS, tt * P:(tt + 1) * P], ident[:],
                                            start=False, stop=(n == N - 1), is_transpose=True,
                                            skip_group_check=True)
                last.then_inc(p_used, 1)

            def steps_for(name, b, par, no):
                if name[:2] == "NT":
                    turn_x(b, int(name[2]), no)
                elif name == "NX1":
                    x_proj(par, 0, R, no)
                elif name == "NX2":
                    x_proj(par, R, R + 2 * N, no)
                elif name == "NG":
                    gate(par, no)
                elif name == "NZ0":
                    dt_proj(par, 0, no)

            pe.wait_ge(const_p, 5 + E)
            for name in LEAD_STEPS:
                if name == "NX1":
                    pe.wait_ge(w_const, 8 * 16)
                steps_for(name, 0, 0, step_no(None, name))

            def batch(b, par):
                for j in range(UNITS):
                    name = STEPS.get(j)
                    if name and name[0] == "N":
                        if not is_last(b):
                            steps_for(name, b + 1, 1 - par, step_no(b, name))
                    elif name:
                        dt_proj(par, int(name[1]), step_no(b, name))
                    if j in GROUP_AT:
                        expert(b, par, GROUP_AT[j])
                    add_y(b, j)

            over_batches(pe, batch)


_SHAPES = {"out": (16, 512, 512)}


def kernel(L0_attn_x, L0_attn_x_proj_w, L0_attn_dt_proj_w, L0_attn_dt_proj_b, L0_attn_A_log, L0_attn_D_param,
           L0_ffn_gate_w, L0_ffn_gate_b, L0_ffn_expert_w, L0_ffn_expert_b):
    import numpy as np
    import concourse.bacc as bacc
    from concourse import mybir as mb
    from concourse.bass_utils import run_bass_kernel_spmd

    def lay(a):
        return np.ascontiguousarray(a)

    def by_tile(a):
        a = np.asarray(a)
        return lay(np.moveaxis(a.reshape(a.shape[0] // 128, 128, *a.shape[1:]), 0, 1))

    arrays = {
        "x": lay(L0_attn_x),
        "xw": lay(np.asarray(L0_attn_x_proj_w).T),
        "dw": lay(np.asarray(L0_attn_dt_proj_w).T),
        "db": by_tile(L0_attn_dt_proj_b),
        "alog": by_tile(L0_attn_A_log),
        "dpar": by_tile(L0_attn_D_param),
        "gw": lay(L0_ffn_gate_w),
        "gb": lay(np.asarray(L0_ffn_gate_b).reshape(1, -1)),
        "ew": lay(L0_ffn_expert_w),
        "eb": lay(L0_ffn_expert_b),
    }
    nc = bacc.Bacc("TRN2", target_bir_lowering=False, num_devices=1)
    args = [nc.dram_tensor(f"in_{n}", a.shape, mb.dt.from_np(a.dtype), kind="ExternalInput").ap()
            for n, a in arrays.items()]
    out = nc.dram_tensor("out", _SHAPES["out"], mb.dt.float32, kind="ExternalOutput").ap()
    build(nc, *args, out)
    r = run_bass_kernel_spmd(nc, [{f"in_{n}": a for n, a in arrays.items()}], core_ids=[0])
    return r.results[0]["out"]
```

```python
from contextlib import ExitStack

import concourse.bass as bass
from concourse import mybir

ALU = mybir.AluOpType
ACT = mybir.ActivationFunctionType
F32 = mybir.dt.float32
F32R = mybir.dt.float32r
U32 = mybir.dt.uint32

P = 128
LN_EPS = 1e-5
DA_BANKS = 3
P_SLOTS = 4
QUAD = 4

STEPS = {2: "Z1", 18: "Z2", 34: "Z3", 38: "NT0", 40: "NT1", 42: "NT2", 44: "NT3", 46: "NX1", 47: "NX2",
         49: "NG", 51: "NZ0"}
ACT_LAG = 7
DVE_LAG = 6
GATE_LAG = 6
EXPERTS_FROM = 5
Y_AT = 8
SIG_AT = 8
G_AT = 2
TIMES_G_AT = (11, 12, 14, 15)
LEAD_STEPS = ["NT0", "NT1", "NT2", "NT3", "NX1", "NX2", "NG", "NZ0"]
ORDER = list(STEPS.values())


def build(nc, x, xw, dw, db, alog, dpar, gw, gb, ew, eb, out):
    B, T, D = x.shape
    R = dw.shape[0]
    N = alog.shape[2]
    E = gw.shape[1]
    DT, TT = D // P, T // P
    UNITS = DT * N
    NQ = N // QUAD
    GROUPS = E * TT
    ADDS = (E - 1) * TT
    GROUP_AT = {EXPERTS_FROM + (g * 9) // 5: g for g in range(GROUPS)}

    ctx = ExitStack()
    with ctx:
        def sb(name, shape, dt=F32):
            return ctx.enter_context(nc.sbuf_tensor(name, shape, dt))

        def psum(name, shape):
            return ctx.enter_context(nc.psum_tensor(name, shape, F32))

        def sem(name):
            return ctx.enter_context(nc.semaphore(name))

        w_parts = nc.dram_tensor("w_parts", (E, P, 2 * DT * D), F32, kind="Internal").ap()
        bc_dram = nc.dram_tensor("bc_rows", (B, 2 * N * T), F32, kind="Internal").ap()

        scan_ps = psum("scan_ps", [P, DA_BANKS, T])
        y_ps = psum("y_ps", [P, 2, TT, P])
        exp_ps = psum("exp_ps", [P, 2, D])
        proj_ps = psum("proj_ps", [P, T])

        ident = sb("ident", [P, P])
        ones = sb("ones", [1, P])
        xw_sb = sb("xw_sb", [P, DT, R + 2 * N])
        dw_sb = sb("dw_sb", [P, D])
        db_sb = sb("db_sb", [P, DT])
        a_sb = sb("a_sb", [P, DT, N])
        dpar_sb = sb("dpar_sb", [P, DT])
        gw_sb = sb("gw_sb", [P, DT, E])
        gb_sb = sb("gb_sb", [1, E])
        EB_ROWS = 32 + E
        eb_raw = sb("eb_raw", [EB_ROWS, D])
        eb_sb = sb("eb_sb", [EB_ROWS, D], F32R)
        pick_f = sb("pick_f", [EB_ROWS, E])
        pick = sb("pick", [EB_ROWS, E], F32R)
        iota = sb("iota", [P, E])
        w_sb = sb("w_sb", [P, 2, 2, DT, D], F32R)
        xn = sb("xn", [P, TT, D])
        stats = sb("stats", [P, TT, 6])
        mv = sb("mv", [P, TT, 2])
        vpe = sb("vpe", [P, TT])
        rstd = sb("rstd", [P, TT])
        newt = sb("newt", [P, TT])
        xT = sb("xT", [P, DT, T])
        xh = sb("xh", [P, DT, T], F32R)
        xl = sb("xl", [P, DT, T], F32R)
        dun = sb("dun", [P, T])
        bc_row = sb("bc_row", [2 * N, T])
        b_sb = sb("b_sb", [P, N, T])
        c_sb = sb("c_sb", [P, N, T])
        delta = sb("delta", [P, 2, T])
        u_sb = sb("u_sb", [P, 2, T])
        pad = sb("pad", [P, 1])
        sp_a = sb("sp_a", [P, T])
        sp_r = sb("sp_r", [P, T])
        xD = sb("xD", [P, 2, T])
        dbx = sb("dbx", [P, 2, QUAD, T])
        p_sb = sb("p_sb", [P, P_SLOTS, T])
        logit = sb("logit", [P, TT, E])
        top = sb("top", [P, TT, 8])
        topi = sb("topi", [P, TT, 8], U32)
        topf = sb("topf", [P, TT, 8])
        hot = sb("hot", [P, 2, TT, E])
        half = sb("half", [P, 2, TT, E])
        acc = sb("acc", [P, TT, D])
        relu = sb("relu", [P, 2, D])
        sig = relu
        s_sb = sb("s_sb", [P, TT, D])
        xo = sb("xo", [P, 2, D])

        w_const = sem("w_const")
        x_in = sem("x_in")
        w_in = [sem("w_in0"), sem("w_in1")]
        b_in = [sem(f"b_in{q}") for q in range(NQ)]
        c_in = [sem(f"c_in{q}") for q in range(NQ)]
        xo_in = [sem("xo_in0"), sem("xo_in1")]
        bc_out = sem("bc_out")
        out_st = [sem("out_st0"), sem("out_st1")]
        const_p = sem("const_p")
        a_exp = sem("a_exp")
        a_ready = sem("a_ready")
        bn_part = sem("bn_part")
        bn_done = sem("bn_done")
        ln_act = sem("ln_act")
        xn_ready = sem("xn_ready")
        proj_done = sem("proj_done")
        proj_used = sem("proj_used")
        sp_step = sem("sp_step")
        sp_ready = sem("sp_ready")
        xd_ready = sem("xd_ready")
        delta_ready = sem("delta_ready")
        u_ready = sem("u_ready")
        gate_step = sem("gate_step")
        half_ready = sem("half_ready")
        da_ready = sem("da_ready")
        dbx_ready = sem("dbx_ready")
        scanned = sem("scanned")
        p_ready = sem("p_ready")
        p_used = sem("p_used")
        y_used = sem("y_used")
        xh_ready = sem("xh_ready")
        xl_ready = sem("xl_ready")
        eb_step = sem("eb_step")
        w_raw = [sem("w_raw0"), sem("w_raw1")]
        wh_done = sem("wh_done")
        wl_done = sem("wl_done")
        w_kept = [sem("w_kept0"), sem("w_kept1")]
        e_done = sem("e_done")
        e_used = sem("e_used")
        e_added = sem("e_added")
        sig_step = sem("sig_step")
        sig_ready = sem("sig_ready")
        g_ready = sem("g_ready")
        sg_done = sem("sg_done")
        out_sum = sem("out_sum")

        def from_start(count):
            return max(count, 0) if isinstance(count, int) else count

        def is_last(b):
            return isinstance(b, int) and b == B - 1

        def is_first(b):
            return isinstance(b, int) and b == 0

        def step_no(b, name):
            if b is None:
                return LEAD_STEPS.index(name)
            order = [s for s in ORDER if s[0] != "N"] if is_last(b) else ORDER
            return b * len(ORDER) + (len(LEAD_STEPS) + order.index(name))

        def t_copied(b, dt):
            if isinstance(b, int) and b == 0:
                return step_no(None, f"NT{dt}") + 1
            return step_no(b - 1, f"NT{dt}") + 1

        block = ctx.enter_context(nc.Block())

        def over_batches(eng, body):
            body(0, 0)
            body(1, 1)
            with eng.Fori(1, B // 2 - 1) as i:
                body(i * 2, 0)
                body(i * 2 + 1, 1)
            body(B - 2, 0)
            body(B - 1, 1)

        @block.sync
        def _(sp):
            def load_x(b):
                sp.dma_start(xn[:], x[bass.ds(b, 1)].rearrange("a (t p) d -> p (a t) d", p=P)).then_inc(x_in, 16)

            def send_bc(b, no):
                sp.wait_ge(proj_used, no + 1)
                sp.dma_start(bc_dram[bass.ds(b, 1), :].rearrange("a (r t) -> (a r) t", t=T),
                             bc_row[:]).then_inc(bc_out, 16)

            def load_bc(b, q, which):
                dst, s, base = (b_sb, b_in, 0) if which == "b" else (c_sb, c_in, N * T)
                src = bc_dram[bass.ds(b, 1), base + q * QUAD * T:base + (q + 1) * QUAD * T]
                src = src.rearrange("a f -> (a f)").partition_broadcast(P)
                sp.dma_start(dst[:, q * QUAD:(q + 1) * QUAD, :].rearrange("p n t -> p (n t)"),
                             src).then_inc(s[q], 16)

            def load_w(e):
                sp.dma_start(w_sb[:, e % 2].rearrange("p h c o -> p (h c o)").bitcast(F32), w_parts[e]).then_inc(w_in[e % 2], 16)

            def load_raw(e):
                for c in range(DT):
                    sp.wait_ge(wl_done, from_start(e * DT + c - 1))
                    sp.dma_start(xo[:, c % 2], ew[e, c * P:(c + 1) * P, :]).then_inc(w_raw[c % 2], 16)

            def keep_parts(e):
                sp.wait_ge(wl_done, (e + 1) * DT)
                sp.dma_start(w_parts[e], w_sb[:, e % 2].rearrange("p h c o -> p (h c o)").bitcast(F32)).then_inc(w_kept[e % 2], 16)

            load_x(0)
            for dst, src in ((xw_sb[:], xw.rearrange("(c k) r -> k c r", k=P)), (dw_sb[:], dw),
                             (db_sb[:], db), (a_sb[:], alog), (dpar_sb[:], dpar),
                             (gw_sb[:], gw.rearrange("(c k) e -> k c e", k=P)), (gb_sb[:], gb),
                             (eb_raw[0:E, :], eb), (eb_raw[32:32 + E, :], eb)):
                sp.dma_start(dst, src).then_inc(w_const, 16)
            sp.wait_ge(proj_done, step_no(None, "NT3") + 1)
            load_x(1)
            send_bc(0, step_no(None, "NX2"))
            sp.wait_ge(bc_out, 16)
            for q in range(NQ):
                load_bc(0, q, "b")
                load_bc(0, q, "c")

            def load_xo(b, tt):
                sp.wait_ge(out_st[tt % 2], (b * 2 + tt // 2) * 16)
                sp.dma_start(xo[:, tt % 2], x[bass.ds(b, 1), tt * P:(tt + 1) * P, :].rearrange("a p d -> (a p) d")
                             ).then_inc(xo_in[tt % 2], 16)

            def store(b, tt):
                sp.wait_ge(out_sum, b * TT + tt + 1)
                sp.dma_start(out[bass.ds(b, 1), tt * P:(tt + 1) * P, :].rearrange("a p d -> (a p) d"),
                             xo[:, tt % 2]).then_inc(out_st[tt % 2], 16)

            def batch(b, par):
                if is_first(b):
                    for e in range(E):
                        load_raw(e)
                        keep_parts(e)
                    more_input(b)
                else:
                    for tt in range(2):
                        load_xo(b - 1, tt)
                    for e in range(2, E):
                        sp.wait_ge(e_done, b * GROUPS + (e - 1) * TT)
                        load_w(e)
                        if e == 3:
                            for tt in range(2):
                                store(b - 1, tt)
                                load_xo(b - 1, tt + 2)
                        if e == 4:
                            for tt in range(2, TT):
                                store(b - 1, tt)
                        if e == 6 and not is_last(b):
                            more_input(b)
                if not is_last(b):
                    sp.wait_ge(bc_out, (b + 2) * 16)
                    for q in range(NQ):
                        sp.wait_ge(dbx_ready, b * DT * NQ + (DT - 1) * NQ + q + 1)
                        load_bc(b + 1, q, "b")
                        sp.wait_ge(p_ready, b * UNITS + (DT - 1) * N + (q + 1) * QUAD)
                        load_bc(b + 1, q, "c")
                    for e in range(2):
                        sp.wait_ge(e_done, (b + 1) * GROUPS - (1 - e) * TT)
                        if is_first(b):
                            sp.wait_ge(w_kept[e], E // 2 * 16)
                        load_w(e)

            def more_input(b):
                if not (isinstance(b, int) and b == B - 2):
                    sp.wait_ge(proj_done, step_no(b, "NT3") + 1)
                    load_x(b + 2)
                send_bc(b + 1, step_no(b, "NX2"))

            over_batches(sp, batch)
            for tt in range(2):
                load_xo(B - 1, tt)
            for tt in range(2):
                store(B - 1, tt)
                load_xo(B - 1, tt + 2)
            for tt in range(2, TT):
                store(B - 1, tt)
            for tt in range(2):
                sp.wait_ge(out_st[tt], B * 2 * 16)

        @block.gpsimd
        def _(pool):
            nc.gpsimd.memset(ones[:], 1.0).then_inc(const_p, 1)
            nc.gpsimd.memset(ident[:], 0.0).then_inc(const_p, 1)
            nc.gpsimd.memset(pick_f[:], 0.0).then_inc(const_p, 1)
            for e in range(E):
                nc.gpsimd.memset(iota[:, e:e + 1], float(e)).then_inc(const_p, 1)
            pool.wait_ge(const_p, 3 + E)
            nc.gpsimd.affine_select(out=ident[:], in_=ident[:], compare_op=ALU.not_equal, fill=1.0,
                                    base=0, pattern=[[-1, P]], channel_multiplier=1).then_inc(const_p, 1)
            for half_no in range(2):
                pool.wait_ge(const_p, 4 + E + half_no)
                nc.gpsimd.affine_select(out=pick_f[:], in_=pick_f[:], compare_op=ALU.not_equal, fill=1.0,
                                        base=-32 * half_no, pattern=[[-1, E]],
                                        channel_multiplier=1).then_inc(const_p, 1)

            def dbx_quad(b, j):
                dt, q = j // NQ, j % NQ
                if q == 0:
                    pool.wait_ge(u_ready, b * DT + dt + 1)
                if dt == 0:
                    pool.wait_ge(b_in[q], (b + 1) * 16)
                pool.wait_ge(scanned, from_start((b * DT * NQ + j - 1) * QUAD))
                nc.gpsimd.tensor_tensor(dbx[:, j % 2], b_sb[:, q * QUAD:(q + 1) * QUAD, :],
                                        u_sb[:, dt % 2, :].unsqueeze(1).to_broadcast([P, QUAD, T]),
                                        ALU.mult).then_inc(dbx_ready, 1)

            def gate_value(b, tt):
                if tt % 2 == 0:
                    pool.wait_ge(sig_ready, b * 2 + tt // 2 + 1)
                nc.gpsimd.tensor_tensor(acc[:, tt], acc[:, tt], sig[:, tt % 2], ALU.mult).then_inc(g_ready, 1)

            def add_x(b, tt):
                pool.wait_ge(sg_done, b * TT + tt + 1)
                pool.wait_ge(xo_in[tt % 2], (b * 2 + tt // 2 + 1) * 16)
                nc.gpsimd.tensor_tensor(xo[:, tt % 2], xo[:, tt % 2], s_sb[:, tt], ALU.add).then_inc(out_sum, 1)

            def batch(b, par):
                for j in range(DT * NQ):
                    dbx_quad(b, j)
                    if not is_first(b):
                        if j in (G_AT, G_AT + 1):
                            gate_value(b - 1, 2 * (j - G_AT))
                            gate_value(b - 1, 2 * (j - G_AT) + 1)
                        if G_AT + 2 <= j < G_AT + 2 + TT:
                            add_x(b - 1, j - G_AT - 2)

            over_batches(pool, batch)
            for tt in range(TT):
                gate_value(B - 1, tt)
            for tt in range(TT):
                add_x(B - 1, tt)

        @block.scalar
        def _(act):
            def ln_root(b):
                act.wait_ge(bn_done, b * 8 + 3)
                nc.scalar.activation(rstd[:], vpe[:], ACT.Ln).then_inc(ln_act, 1)
                act.wait_ge(ln_act, b * 2 + 1)
                nc.scalar.activation(rstd[:], rstd[:], ACT.Exp, scale=-0.5).then_inc(ln_act, 1)

            def copy_t(b, dt, no):
                act.wait_ge(proj_done, no + 1)
                if dt == 0:
                    act.wait_ge(u_ready, b * DT)
                    act.wait_ge(xd_ready, b * DT)
                    act.wait_ge(xl_ready, b * DT)
                nc.scalar.activation(xT[:, dt, :], proj_ps[:], ACT.Copy).then_inc(proj_used, 1)

            def split_x(b, dt):
                act.wait_ge(proj_used, t_copied(b, dt))
                act.wait_ge(e_done, b * GROUPS)
                act.wait_ge(xl_ready, from_start((b - 1) * DT + dt + 1))
                nc.scalar.activation(xh[:, dt, :], xT[:, dt, :], ACT.Copy).then_inc(xh_ready, 1)

            def copy_dun(no):
                act.wait_ge(proj_done, no + 1)
                nc.scalar.activation(dun[:], proj_ps[:], ACT.Copy).then_inc(proj_used, 1)

            def copy_bc(b, no):
                act.wait_ge(proj_done, no + 1)
                act.wait_ge(bc_out, b * 16)
                nc.scalar.activation(bc_row[:], proj_ps[0:2 * N, :], ACT.Copy).then_inc(proj_used, 1)

            def softplus(b, dt, no):
                k = b * DT + dt
                act.wait_ge(proj_done, no + 1)
                act.wait_ge(delta_ready, k)
                bias = db_sb[:, dt:dt + 1]
                nc.scalar.activation(sp_a[:], proj_ps[:], ACT.Abs, bias=bias).then_inc(sp_step, 1)
                nc.scalar.activation(sp_r[:], proj_ps[:], ACT.Relu, bias=bias).then_inc(proj_used, 1)
                act.wait_ge(sp_step, k * 2 + 1)
                nc.scalar.activation(sp_a[:], sp_a[:], ACT.Exp, scale=-1.0).then_inc(sp_step, 1)
                act.wait_ge(proj_used, t_copied(b, dt))
                act.wait_ge(p_used, from_start((k - 2) * N + 1))
                nc.scalar.activation(xD[:, dt % 2, :], xT[:, dt, :], ACT.Copy,
                                     scale=dpar_sb[:, dt:dt + 1]).then_inc(xd_ready, 1)
                act.wait_ge(sp_step, k * 2 + 2)
                nc.scalar.activation(sp_a[:], sp_a[:], ACT.Ln, bias=1.0).then_inc(sp_ready, 1)

            def da_unit(b, par, j):
                dt, n = j // N, j % N
                u = b * UNITS + j
                if n == 0:
                    act.wait_ge(delta_ready, b * DT + dt + 1)
                back = DA_BANKS if j >= DA_BANKS else (1 if j == 0 else DA_BANKS + 1)
                act.wait_ge(p_ready, from_start(u - back + 1))
                nc.scalar.activation(scan_ps[:, j % DA_BANKS, :], delta[:, dt % 2, :], ACT.Exp,
                                     scale=a_sb[:, dt, n:n + 1]).then_inc(da_ready, 1)

            def copy_y(b, dt):
                k = b * DT + dt
                act.wait_ge(p_used, (k + 1) * N)
                act.wait_ge(out_sum, b * TT)
                nc.scalar.activation(s_sb[:, :, dt * P:(dt + 1) * P], y_ps[:, dt % 2], ACT.Copy).then_inc(y_used, 1)

            def expert_relu(b, par, g):
                e, tt = g // TT, g % TT
                G = b * GROUPS + g
                act.wait_ge(e_done, G + 1)
                if g == 0:
                    act.wait_ge(half_ready, b + 1)
                if e == 0:
                    act.wait_ge(sg_done, from_start((b - 1) * TT + tt + 1))
                    dst = acc[:, tt]
                else:
                    a = b * ADDS + g - TT
                    act.wait_ge(e_added, from_start(a - 1))
                    act.wait_ge(g_ready, b * TT)
                    dst = relu[:, g % 2]
                nc.scalar.activation(dst, exp_ps[:, g % 2], ACT.Relu,
                                     scale=half[:, par, tt, e:e + 1]).then_inc(e_used, 1)

            def sigmoid(b, pair, part):
                c = (b * 2 + pair) * 2
                src = acc[:, 2 * pair:2 * pair + 2]
                if part == 0:
                    act.wait_ge(e_added, (b + 1) * ADDS)
                    act.wait_ge(g_ready, b * TT + 2 * pair)
                    nc.scalar.activation(sig[:], src, ACT.Exp, scale=-1.0).then_inc(sig_step, 1)
                if part == 1:
                    act.wait_ge(sig_step, c + 1)
                    nc.scalar.activation(sig[:], sig[:], ACT.Ln, bias=1.0).then_inc(sig_step, 1)
                if part == 2:
                    act.wait_ge(sig_step, c + 2)
                    nc.scalar.activation(sig[:], sig[:], ACT.Exp, scale=-1.0).then_inc(sig_ready, 1)

            act.add_instruction(mybir.InstLoadActFuncSet(
                name=nc.get_next_instruction_name(), act_func_set_id=6,
                engine=mybir.EngineType.Activation))
            ln_root(0)
            act.wait_ge(w_const, 9 * 16)
            nc.scalar.activation(a_sb[:], a_sb[:], ACT.Exp).then_inc(a_exp, 1)
            for dt in range(DT):
                copy_t(0, dt, step_no(None, f"NT{dt}"))
            copy_dun(step_no(None, "NX1"))
            copy_bc(0, step_no(None, "NX2"))
            softplus(0, 0, step_no(None, "NZ0"))
            act.wait_ge(a_ready, 1)

            def batch(b, par):
                nxt = not is_last(b)
                for j in range(UNITS):
                    if j == 20 and nxt:
                        ln_root(b + 1)
                    name = STEPS.get(j - ACT_LAG + 1)
                    if name and (nxt or name[0] != "N"):
                        no = step_no(b, name)
                        if name[:2] == "NT":
                            copy_t(b + 1, int(name[2]), no)
                        elif name == "NX1":
                            copy_dun(no)
                        elif name == "NX2":
                            copy_bc(b + 1, no)
                        elif name == "NZ0":
                            softplus(b + 1, 0, no)
                        elif name[0] == "Z":
                            softplus(b, int(name[1]), no)
                    if j - ACT_LAG in GROUP_AT:
                        expert_relu(b, par, GROUP_AT[j - ACT_LAG])
                    if j - ACT_LAG + UNITS in GROUP_AT and not is_first(b):
                        expert_relu(b - 1, 1 - par, GROUP_AT[j - ACT_LAG + UNITS])
                    if j == 2:
                        for dt in range(DT):
                            split_x(b, dt)
                    if j == Y_AT and not is_first(b):
                        copy_y(b - 1, DT - 1)
                    if j % N == 12 and j >= N:
                        copy_y(b, j // N - 1)
                    if not is_first(b) and SIG_AT <= j < SIG_AT + 6:
                        sigmoid(b - 1, (j - SIG_AT) // 3, (j - SIG_AT) % 3)
                    da_unit(b, par, j)

            over_batches(act, batch)
            for j in range(ACT_LAG):
                if j - ACT_LAG + UNITS in GROUP_AT:
                    expert_relu(B - 1, 1, GROUP_AT[j - ACT_LAG + UNITS])
            copy_y(B - 1, DT - 1)
            for pair in range(2):
                for part in range(3):
                    sigmoid(B - 1, pair, part)

        @block.vector
        def _(dve):
            def ln_stats(b, tt):
                dve.wait_ge(x_in, (b + 1) * 16)
                nc.vector.bn_stats(stats[:, tt, :], xn[:, tt, :]).then_inc(bn_done if tt == TT - 1 else bn_part, 1)

            def ln_var(b):
                dve.wait_ge(bn_part, (b + 1) * (TT - 1))
                dve.wait_ge(bn_done, b * 8 + 1)
                nc.vector.memset(pad[:], 0.0)
                for tt in range(TT):
                    last = nc.vector.bn_aggr(mv[:, tt, :], stats[:, tt, :])
                last.then_inc(bn_done, 1)
                dve.wait_ge(bn_done, b * 8 + 2)
                nc.vector.tensor_scalar(vpe[:], mv[:, :, 1], LN_EPS, None, ALU.add).then_inc(bn_done, 1)

            def ln_newton(b):
                dve.wait_ge(ln_act, b * 2 + 2)
                c = b * 8 + 3
                nc.vector.tensor_tensor(newt[:], rstd[:], rstd[:], ALU.mult).then_inc(bn_done, 1)
                dve.wait_ge(bn_done, c + 1)
                nc.vector.tensor_tensor(newt[:], newt[:], vpe[:], ALU.mult).then_inc(bn_done, 1)
                dve.wait_ge(bn_done, c + 2)
                nc.vector.tensor_scalar(newt[:], newt[:], -0.5, 1.5, ALU.mult, ALU.add).then_inc(bn_done, 1)
                dve.wait_ge(bn_done, c + 3)
                nc.vector.tensor_tensor(rstd[:], rstd[:], newt[:], ALU.mult).then_inc(bn_done, 1)
                dve.wait_ge(bn_done, c + 4)

            def ln_apply(b, tt):
                inst = nc.vector.tensor_scalar(xn[:, tt, :], xn[:, tt, :], mv[:, tt, 0:1], rstd[:, tt:tt + 1],
                                               ALU.subtract, ALU.mult)
                if tt == TT - 1:
                    inst.then_inc(bn_done, 1)
                else:
                    inst.then_inc(xn_ready, 1)

            def delta_u(b, dt):
                k = b * DT + dt
                dve.wait_ge(sp_ready, k + 1)
                dve.wait_ge(proj_used, t_copied(b, dt))
                dve.wait_ge(da_ready, from_start((k - 1) * N))
                nc.vector.tensor_tensor(delta[:, dt % 2, :], sp_a[:], sp_r[:], ALU.add).then_inc(delta_ready, 1)
                dve.wait_ge(delta_ready, k + 1)
                dve.wait_ge(dbx_ready, from_start((k - 1) * NQ))
                nc.vector.tensor_tensor(u_sb[:, dt % 2, :], delta[:, dt % 2, :], xT[:, dt, :],
                                        ALU.mult).then_inc(u_ready, 1)

            def split_x(b, dt):
                dve.wait_ge(xh_ready, b * DT + dt + 1)
                nc.vector.tensor_tensor(xl[:, dt, :], xT[:, dt, :], xh[:, dt, :].bitcast(F32),
                                        ALU.subtract).then_inc(xl_ready, 1)

            def split_w(e, c):
                dve.wait_ge(w_raw[c % 2], (e * (DT // 2) + c // 2 + 1) * 16)
                if c == 0:
                    dve.wait_ge(e_done, from_start((e - 1) * TT))
                    dve.wait_ge(w_kept[e % 2], e // 2 * 16)
                high = w_sb[:, e % 2, 0, c, :]
                nc.vector.tensor_copy(high, xo[:, c % 2]).then_inc(wh_done, 1)
                dve.wait_ge(wh_done, e * DT + c + 1)
                nc.vector.tensor_tensor(w_sb[:, e % 2, 1, c, :], xo[:, c % 2], high.bitcast(F32),
                                        ALU.subtract).then_inc(wl_done, 1)

            GATE_CHAIN = 4

            def gate(b, par, no):
                dve.wait_ge(proj_done, no + 1)
                nc.vector.tensor_copy(logit[:], proj_ps[:, 0:TT * E].rearrange("p (t e) -> p t e", e=E)
                                      ).then_inc(proj_used, 1)
                dve.wait_ge(proj_used, no + 1)
                nc.vector.memset(pad[:], 0.0)
                c = b * GATE_CHAIN
                for tt in range(TT):
                    last = nc.vector.max(top[:, tt, :], logit[:, tt, :])
                last.then_inc(gate_step, 1)
                dve.wait_ge(gate_step, c + 1)
                nc.vector.memset(pad[:], 0.0)
                for tt in range(TT):
                    last = nc.vector.max_index(topi[:, tt, :], top[:, tt, :], logit[:, tt, :])
                last.then_inc(gate_step, 1)
                dve.wait_ge(gate_step, c + 2)
                nc.vector.tensor_copy(topf[:], topi[:]).then_inc(gate_step, 1)
                dve.wait_ge(gate_step, c + 3)
                for tt in range(TT):
                    for s in range(2):
                        last = nc.vector.tensor_scalar(hot[:, s, tt, :], iota[:], topf[:, tt, s:s + 1], 0.5,
                                                       ALU.is_equal, ALU.mult)
                last.then_inc(gate_step, 1)
                dve.wait_ge(gate_step, c + 4)
                dve.wait_ge(e_used, from_start((b - 1) * GROUPS))
                nc.vector.tensor_tensor(half[:, par], hot[:, 0], hot[:, 1], ALU.add).then_inc(half_ready, 1)

            def scan(b, j):
                u = b * UNITS + j
                dve.wait_ge(da_ready, u + 1)
                if j % QUAD == 0:
                    dve.wait_ge(dbx_ready, b * DT * NQ + j // QUAD + 1)
                bank = scan_ps[:, j % DA_BANKS, :]
                nc.vector.tensor_tensor_scan(bank, bank, dbx[:, (j // QUAD) % 2, j % QUAD, :], 0.0,
                                             ALU.mult, ALU.add).then_inc(scanned, 1)

            def times_c(b, j):
                dt, n = j // N, j % N
                u = b * UNITS + j
                dve.wait_ge(scanned, u + 1)
                if dt == 0 and n % QUAD == 0:
                    dve.wait_ge(c_in[n // QUAD], (b + 1) * 16)
                dve.wait_ge(p_used, from_start(u - P_SLOTS + 1))
                nc.vector.tensor_tensor(p_sb[:, j % P_SLOTS, :], scan_ps[:, j % DA_BANKS, :], c_sb[:, n, :],
                                        ALU.mult).then_inc(p_ready, 1)

            def expert_add(b, g):
                tt = g % TT
                a = b * ADDS + g - TT
                dve.wait_ge(e_used, b * GROUPS + g + 1)
                dve.wait_ge(e_added, from_start(a - TT + 1))
                nc.vector.tensor_tensor(acc[:, tt], acc[:, tt], relu[:, g % 2], ALU.add).then_inc(e_added, 1)

            def times_g(b, tt):
                dve.wait_ge(y_used, (b + 1) * DT)
                dve.wait_ge(g_ready, b * TT + tt + 1)
                nc.vector.tensor_tensor(s_sb[:, tt], s_sb[:, tt], acc[:, tt], ALU.mult).then_inc(sg_done, 1)

            for tt in range(TT):
                ln_stats(0, tt)
            ln_var(0)
            ln_newton(0)
            for tt in range(TT):
                ln_apply(0, tt)
            dve.wait_ge(a_exp, 1)
            nc.vector.tensor_scalar(a_sb[:], a_sb[:], -1.0, None, ALU.mult).then_inc(a_ready, 1)
            dve.wait_ge(const_p, 6 + E)
            nc.vector.tensor_copy(pick[:], pick_f[:]).then_inc(eb_step, 1)
            nc.vector.memset(eb_sb[:].bitcast(F32), 0.0).then_inc(eb_step, 1)
            dve.wait_ge(eb_step, 2)
            dve.wait_ge(w_const, 9 * 16)
            for lo in (0, 32):
                nc.vector.tensor_copy(eb_sb[lo:lo + E, :], eb_raw[lo:lo + E, :]).then_inc(eb_step, 1)
            dve.wait_ge(eb_step, 4)
            nc.vector.tensor_tensor(eb_sb[32:32 + E, :], eb_raw[32:32 + E, :], eb_sb[32:32 + E, :].bitcast(F32),
                                    ALU.subtract).then_inc(eb_step, 1)
            gate(0, 0, step_no(None, "NG"))
            delta_u(0, 0)

            def batch(b, par):
                nxt = not is_last(b)
                for j in range(UNITS):
                    scan(b, j)
                    if nxt:
                        if j in (15, 16):
                            ln_stats(b + 1, 2 * (j - 15))
                            ln_stats(b + 1, 2 * (j - 15) + 1)
                        if j == 17:
                            ln_var(b + 1)
                        if j == 21:
                            ln_newton(b + 1)
                        if j in (22, 24):
                            ln_apply(b + 1, j - 22)
                            ln_apply(b + 1, j - 21)
                    if j in (1, 2, 3, 4):
                        split_x(b, j - 1)
                    if is_first(b):
                        if j == 5:
                            for c in range(DT):
                                split_w(0, c)
                        if j >= 10 and (j - 3) % 7 < DT and (j - 3) // 7 < E:
                            split_w((j - 3) // 7, (j - 3) % 7)
                    name = STEPS.get(j - GATE_LAG)
                    if name == "NG" and nxt:
                        gate(b + 1, 1 - par, step_no(b, name))
                    name = STEPS.get(j - DVE_LAG)
                    if name and name[0] == "Z":
                        delta_u(b, int(name[1]))
                    if name == "NZ0" and nxt:
                        delta_u(b + 1, 0)
                    if j - DVE_LAG + UNITS in GROUP_AT and not is_first(b):
                        expert_add(b - 1, GROUP_AT[j - DVE_LAG + UNITS])
                    if j - DVE_LAG in GROUP_AT and GROUP_AT[j - DVE_LAG] >= TT:
                        expert_add(b, GROUP_AT[j - DVE_LAG])
                    if not is_first(b) and j in TIMES_G_AT:
                        times_g(b - 1, TIMES_G_AT.index(j))
                    if j >= 1:
                        times_c(b, j - 1)
                times_c(b, UNITS - 1)

            over_batches(dve, batch)
            for j in range(DVE_LAG):
                if j - DVE_LAG + UNITS in GROUP_AT:
                    expert_add(B - 1, GROUP_AT[j - DVE_LAG + UNITS])
            for tt in range(TT):
                times_g(B - 1, tt)

        @block.tensor
        def _(pe):
            def bank_free(no):
                pe.wait_ge(proj_used, no)

            def turn_x(b, dt, no):
                bank_free(no)
                if dt == 0:
                    pe.wait_ge(bn_done, (b + 1) * 8)
                    pe.wait_ge(xn_ready, (b + 1) * (TT - 1))
                for tt in range(TT):
                    last = nc.tensor.matmul(proj_ps[:, tt * P:(tt + 1) * P], xn[:, tt, dt * P:(dt + 1) * P],
                                            ident[:], start=True, stop=True, is_transpose=True)
                last.then_inc(proj_done, 1)

            def x_proj(lo, hi, no):
                bank_free(no)
                for c in range(DT):
                    last = nc.tensor.matmul(proj_ps[0:hi - lo, :], xw_sb[:, c, lo:hi], xT[:, c, :],
                                            start=(c == 0), stop=(c == DT - 1))
                last.then_inc(proj_done, 1)

            def dt_proj(dt, no):
                bank_free(no)
                nc.tensor.matmul(proj_ps[:], dw_sb[:, dt * P:(dt + 1) * P], dun[:],
                                 start=True, stop=True).then_inc(proj_done, 1)

            def gate(no):
                bank_free(no)
                for tt in range(TT):
                    dst = proj_ps[:, tt * E:(tt + 1) * E]
                    for c in range(DT):
                        nc.tensor.matmul(dst, xT[:, c, tt * P:(tt + 1) * P], gw_sb[:, c, :],
                                         start=(c == 0), stop=False)
                    last = nc.tensor.matmul(dst, ones[:], gb_sb[:], start=False, stop=True)
                last.then_inc(proj_done, 1)

            def expert(b, g):
                e, tt = g // TT, g % TT
                if g == 0:
                    pe.wait_ge(xl_ready, (b + 1) * DT)
                if tt == 0 and is_first(b):
                    pe.wait_ge(wl_done, (e + 1) * DT)
                elif tt == 0:
                    pe.wait_ge(w_in[e % 2], ((b - 1) * (E // 2) + e // 2 + 1) * 16)
                pe.wait_ge(e_used, from_start(b * GROUPS + g - 1))
                dst = exp_ps[:, g % 2]
                w_high, w_low = w_sb[:, e % 2, 0], w_sb[:, e % 2, 1]
                for c in range(DT):
                    high, low = xh[:, c, tt * P:(tt + 1) * P], xl[:, c, tt * P:(tt + 1) * P]
                    nc.tensor.matmul(dst, high, w_high[:, c, :], start=(c == 0), stop=False)
                    nc.tensor.matmul(dst, high, w_low[:, c, :], start=False, stop=False)
                    nc.tensor.matmul(dst, low, w_high[:, c, :], start=False, stop=False)
                nc.tensor.matmul(dst, pick[:, e:e + 1].to_broadcast([EB_ROWS, P]), eb_sb[:],
                                 start=False, stop=True).then_inc(e_done, 1)

            def add_y(b, j):
                dt, n = j // N, j % N
                k = b * DT + dt
                y = y_ps[:, dt % 2]
                if n == 0:
                    pe.wait_ge(y_used, from_start(k - 1))
                    pe.wait_ge(xd_ready, k + 1)
                    for tt in range(TT):
                        nc.tensor.matmul(y[:, tt, :], xD[:, dt % 2, tt * P:(tt + 1) * P], ident[:],
                                         start=(tt == 0), stop=False, is_transpose=True, skip_group_check=True)
                pe.wait_ge(p_ready, b * UNITS + j + 1)
                for tt in range(TT):
                    last = nc.tensor.matmul(y[:, tt, :], p_sb[:, j % P_SLOTS, tt * P:(tt + 1) * P], ident[:],
                                            start=False, stop=(n == N - 1), is_transpose=True,
                                            skip_group_check=True)
                last.then_inc(p_used, 1)

            def steps_for(name, b, no):
                if name[:2] == "NT":
                    turn_x(b, int(name[2]), no)
                elif name == "NX1":
                    x_proj(0, R, no)
                elif name == "NX2":
                    x_proj(R, R + 2 * N, no)
                elif name == "NG":
                    gate(no)
                elif name == "NZ0":
                    dt_proj(0, no)

            pe.wait_ge(const_p, 6 + E)
            pe.wait_ge(eb_step, 5)
            for name in LEAD_STEPS:
                if name == "NX1":
                    pe.wait_ge(w_const, 9 * 16)
                steps_for(name, 0, step_no(None, name))

            def batch(b, par):
                for j in range(UNITS):
                    name = STEPS.get(j)
                    if name and name[0] == "N":
                        if not is_last(b):
                            steps_for(name, b + 1, step_no(b, name))
                    elif name:
                        dt_proj(int(name[1]), step_no(b, name))
                    if j in GROUP_AT:
                        expert(b, GROUP_AT[j])
                    add_y(b, j)

            over_batches(pe, batch)


_SHAPES = {"out": (16, 512, 512)}


def kernel(L0_attn_x, L0_attn_x_proj_w, L0_attn_dt_proj_w, L0_attn_dt_proj_b, L0_attn_A_log, L0_attn_D_param,
           L0_ffn_gate_w, L0_ffn_gate_b, L0_ffn_expert_w, L0_ffn_expert_b):
    import numpy as np
    import concourse.bacc as bacc
    from concourse import mybir as mb
    from concourse.bass_utils import run_bass_kernel_spmd

    def lay(a):
        return np.ascontiguousarray(a)

    def by_tile(a):
        a = np.asarray(a)
        return lay(np.moveaxis(a.reshape(a.shape[0] // 128, 128, *a.shape[1:]), 0, 1))

    arrays = {
        "x": lay(L0_attn_x),
        "xw": lay(np.asarray(L0_attn_x_proj_w).T),
        "dw": lay(np.asarray(L0_attn_dt_proj_w).T),
        "db": by_tile(L0_attn_dt_proj_b),
        "alog": by_tile(L0_attn_A_log),
        "dpar": by_tile(L0_attn_D_param),
        "gw": lay(L0_ffn_gate_w),
        "gb": lay(np.asarray(L0_ffn_gate_b).reshape(1, -1)),
        "ew": lay(L0_ffn_expert_w),
        "eb": lay(L0_ffn_expert_b),
    }
    nc = bacc.Bacc("TRN2", target_bir_lowering=False, num_devices=1)
    args = [nc.dram_tensor(f"in_{n}", a.shape, mb.dt.from_np(a.dtype), kind="ExternalInput").ap()
            for n, a in arrays.items()]
    out = nc.dram_tensor("out", _SHAPES["out"], mb.dt.float32, kind="ExternalOutput").ap()
    build(nc, *args, out)
    r = run_bass_kernel_spmd(nc, [{f"in_{n}": a for n, a in arrays.items()}], core_ids=[0])
    return r.results[0]["out"]
```

```python
from contextlib import ExitStack

import concourse.bass as bass
from concourse import mybir

ALU = mybir.AluOpType
ACT = mybir.ActivationFunctionType
F32 = mybir.dt.float32
F32R = mybir.dt.float32r
U32 = mybir.dt.uint32

P = 128
LN_EPS = 1e-5
DA_BANKS = 3
P_SLOTS = 6
QUAD = 4

STEPS = {2: "Z1", 18: "Z2", 34: "Z3", 38: "NT0", 40: "NT1", 42: "NT2", 44: "NT3", 45: "NX0", 47: "NX1",
         49: "NR", 50: "NS", 52: "NZ0"}
ACT_LAG = 7
DVE_LAG = 6
XD_AT = 11
XD_ADD_AT = 2
GATE_LAG = 6
EXPERTS_FROM = 4
Y_AT = 7
SIG_AT = 7
G_AT = 2
TIMES_G_AT = (10, 11, 12, 14)
LEAD_STEPS = ["NT0", "NT1", "NT2", "NT3", "NX0", "NX1", "NR", "NS", "NZ0"]
ORDER = list(STEPS.values())


def build(nc, x, xw, dw, db, alog, dpar, gw, gb, ew, eb, out):
    B, T, D = x.shape
    R = dw.shape[0]
    N = alog.shape[2]
    E = gw.shape[1]
    DT, TT = D // P, T // P
    UNITS = DT * N
    NQ = N // QUAD
    GROUPS = E * TT
    ADDS = (E - 1) * TT
    PROJ = R + 2 * N + E
    GROUP_AT = {EXPERTS_FROM + (g * 9) // 5: g for g in range(GROUPS)}

    ctx = ExitStack()
    with ctx:
        def sb(name, shape, dt=F32):
            return ctx.enter_context(nc.sbuf_tensor(name, shape, dt))

        def psum(name, shape):
            return ctx.enter_context(nc.psum_tensor(name, shape, F32))

        def sem(name):
            return ctx.enter_context(nc.semaphore(name))

        w_parts = nc.dram_tensor("w_parts", (E, P, 2 * DT * D), F32, kind="Internal").ap()
        bc_dram = nc.dram_tensor("bc_rows", (B, 2 * N * T), F32, kind="Internal").ap()

        scan_ps = psum("scan_ps", [P, DA_BANKS, T])
        y_ps = psum("y_ps", [P, 2, TT, P])
        exp_ps = psum("exp_ps", [P, 2, D])
        proj_ps = psum("proj_ps", [P, T])

        ident = sb("ident", [P, P])
        xwg_sb = sb("xwg_sb", [P, DT, R + 2 * N + E])
        dw_sb = sb("dw_sb", [P, D])
        db_sb = sb("db_sb", [P, DT])
        a_sb = sb("a_sb", [P, DT, N])
        dpar_sb = sb("dpar_sb", [P, DT])
        gb_sb = sb("gb_sb", [P, E])
        EB_ROWS = 32 + E
        eb_sb = sb("eb_sb", [EB_ROWS, D], F32R)
        pick_f = sb("pick_f", [EB_ROWS, E])
        pick = sb("pick", [EB_ROWS, E], F32R)
        iota = sb("iota", [P, E])
        w_sb = sb("w_sb", [P, 2, 2, DT, D], F32R)
        xn = sb("xn", [P, TT, D])
        stats = sb("stats", [P, TT, 6])
        mv = sb("mv", [P, TT, 2])
        vpe = sb("vpe", [P, TT])
        rstd = sb("rstd", [P, TT])
        newt = sb("newt", [P, TT])
        xT = sb("xT", [P, DT, T])
        xh = sb("xh", [P, DT, T], F32R)
        xl = sb("xl", [P, DT, T], F32R)
        dun = sb("dun", [P, T])
        bc_row = sb("bc_row", [2 * N, T])
        b_sb = sb("b_sb", [P, N, T])
        c_sb = sb("c_sb", [P, N, T])
        delta = sb("delta", [P, 2, T])
        u_sb = sb("u_sb", [P, 2, T])
        pad = sb("pad", [P, 1])
        xD = sb("xD", [P, T])
        tok = sb("tok", [P, TT, R + 2 * N + E])
        dbx = sb("dbx", [P, 2, QUAD, T])
        p_sb = sb("p_sb", [P, P_SLOTS, T])
        logit = sb("logit", [P, TT, E])
        top = sb("top", [P, TT, 8])
        topi = sb("topi", [P, TT, 8], U32)
        topf = sb("topf", [P, TT, 8])
        hot = sb("hot", [P, 2, TT, E])
        half = sb("half", [P, 2, TT, E])
        acc = sb("acc", [P, TT, D])
        relu = sb("relu", [P, 2, D])
        sig = relu
        s_sb = sb("s_sb", [P, TT, D])
        xo = sb("xo", [P, 2, D])

        w_const = sem("w_const")
        x_in = sem("x_in")
        w_in = [sem("w_in0"), sem("w_in1")]
        b_in = [sem(f"b_in{q}") for q in range(NQ)]
        c_in = [sem(f"c_in{q}") for q in range(NQ)]
        xo_in = [sem("xo_in0"), sem("xo_in1")]
        bc_out = sem("bc_out")
        out_st = [sem("out_st0"), sem("out_st1")]
        const_p = sem("const_p")
        a_exp = sem("a_exp")
        a_ready = sem("a_ready")
        bn_part = sem("bn_part")
        bn_done = sem("bn_done")
        ln_act = sem("ln_act")
        xn_ready = sem("xn_ready")
        proj_done = sem("proj_done")
        proj_used = sem("proj_used")
        sp_step = sem("sp_step")
        sp_ready = sem("sp_ready")
        xd_ready = sem("xd_ready")
        xd_used = sem("xd_used")
        delta_ready = sem("delta_ready")
        u_ready = sem("u_ready")
        gate_step = sem("gate_step")
        half_ready = sem("half_ready")
        da_ready = sem("da_ready")
        dbx_ready = sem("dbx_ready")
        scanned = sem("scanned")
        p_ready = sem("p_ready")
        p_used = sem("p_used")
        y_used = sem("y_used")
        xh_ready = sem("xh_ready")
        xl_ready = sem("xl_ready")
        eb_step = sem("eb_step")
        w_raw = [sem("w_raw0"), sem("w_raw1")]
        wh_done = sem("wh_done")
        wl_done = sem("wl_done")
        w_kept = [sem("w_kept0"), sem("w_kept1")]
        e_done = sem("e_done")
        e_used = sem("e_used")
        e_added = sem("e_added")
        sig_step = sem("sig_step")
        sig_ready = sem("sig_ready")
        g_ready = sem("g_ready")
        sg_done = sem("sg_done")
        out_sum = sem("out_sum")

        def from_start(count):
            return max(count, 0) if isinstance(count, int) else count

        def is_last(b):
            return isinstance(b, int) and b == B - 1

        def is_first(b):
            return isinstance(b, int) and b == 0

        def step_no(b, name):
            if b is None:
                return LEAD_STEPS.index(name)
            order = [s for s in ORDER if s[0] != "N"] if is_last(b) else ORDER
            return b * len(ORDER) + (len(LEAD_STEPS) + order.index(name))

        def t_copied(b, dt):
            if isinstance(b, int) and b == 0:
                return step_no(None, f"NT{dt}") + 1
            return step_no(b - 1, f"NT{dt}") + 1

        def back(j, ring):
            return ring if j >= ring else j + UNITS - max(i for i in range(UNITS) if i % ring == j)

        block = ctx.enter_context(nc.Block())

        def over_batches(eng, body):
            body(0, 0)
            body(1, 1)
            with eng.Fori(1, B // 2 - 1) as i:
                body(i * 2, 0)
                body(i * 2 + 1, 1)
            body(B - 2, 0)
            body(B - 1, 1)

        @block.sync
        def _(sp):
            def load_x(b):
                sp.dma_start(xn[:], x[bass.ds(b, 1)].rearrange("a (t p) d -> p (a t) d", p=P)).then_inc(x_in, 16)

            def send_bc(b, no):
                sp.wait_ge(proj_used, no + 1)
                sp.dma_start(bc_dram[bass.ds(b, 1), :].rearrange("a (r t) -> (a r) t", t=T),
                             bc_row[:]).then_inc(bc_out, 16)

            def load_bc(b, q, which):
                dst, s, base = (b_sb, b_in, 0) if which == "b" else (c_sb, c_in, N * T)
                src = bc_dram[bass.ds(b, 1), base + q * QUAD * T:base + (q + 1) * QUAD * T]
                src = src.rearrange("a f -> (a f)").partition_broadcast(P)
                sp.dma_start(dst[:, q * QUAD:(q + 1) * QUAD, :].rearrange("p n t -> p (n t)"),
                             src).then_inc(s[q], 16)

            def load_w(e):
                sp.dma_start(w_sb[:, e % 2].rearrange("p h c o -> p (h c o)").bitcast(F32), w_parts[e]).then_inc(w_in[e % 2], 16)

            def load_raw(e):
                for c in range(DT):
                    sp.wait_ge(wl_done, from_start(e * DT + c - 1))
                    sp.dma_start(xo[:, c % 2], ew[e, c * P:(c + 1) * P, :]).then_inc(w_raw[c % 2], 16)

            def keep_parts(e):
                sp.wait_ge(wl_done, (e + 1) * DT)
                sp.dma_start(w_parts[e], w_sb[:, e % 2].rearrange("p h c o -> p (h c o)").bitcast(F32)).then_inc(w_kept[e % 2], 16)

            load_x(0)
            for dst, src in ((xwg_sb[:, :, 0:R + 2 * N], xw.rearrange("(c k) r -> k c r", k=P)), (dw_sb[:], dw),
                             (db_sb[:], db), (a_sb[:], alog), (dpar_sb[:], dpar),
                             (xwg_sb[:, :, R + 2 * N:], gw.rearrange("(c k) e -> k c e", k=P)),
                             (gb_sb[:], gb.rearrange("a e -> (a e)").partition_broadcast(P)),
                             (s_sb[0:E, 0, :], eb), (s_sb[32:32 + E, 0, :], eb)):
                sp.dma_start(dst, src).then_inc(w_const, 16)
            sp.wait_ge(proj_done, step_no(None, "NT3") + 1)
            load_x(1)
            send_bc(0, step_no(None, "NS"))
            sp.wait_ge(bc_out, 16)
            for q in range(NQ):
                load_bc(0, q, "b")
                load_bc(0, q, "c")

            def load_xo(b, tt):
                sp.wait_ge(out_st[tt % 2], (b * 2 + tt // 2) * 16)
                sp.dma_start(xo[:, tt % 2], x[bass.ds(b, 1), tt * P:(tt + 1) * P, :].rearrange("a p d -> (a p) d")
                             ).then_inc(xo_in[tt % 2], 16)

            def store(b, tt):
                sp.wait_ge(out_sum, b * TT + tt + 1)
                sp.dma_start(out[bass.ds(b, 1), tt * P:(tt + 1) * P, :].rearrange("a p d -> (a p) d"),
                             xo[:, tt % 2]).then_inc(out_st[tt % 2], 16)

            def batch(b, par):
                if is_first(b):
                    for e in range(E):
                        load_raw(e)
                        keep_parts(e)
                    more_input(b)
                else:
                    for tt in range(2):
                        load_xo(b - 1, tt)
                    for e in range(2, E):
                        sp.wait_ge(e_done, b * GROUPS + (e - 1) * TT)
                        load_w(e)
                        if e == 3:
                            for tt in range(2):
                                store(b - 1, tt)
                                load_xo(b - 1, tt + 2)
                        if e == 4:
                            for tt in range(2, TT):
                                store(b - 1, tt)
                        if e == 6 and not is_last(b):
                            more_input(b)
                if not is_last(b):
                    sp.wait_ge(bc_out, (b + 2) * 16)
                    for q in range(NQ):
                        sp.wait_ge(dbx_ready, b * DT * NQ + (DT - 1) * NQ + q + 1)
                        load_bc(b + 1, q, "b")
                        sp.wait_ge(p_ready, b * UNITS + (DT - 1) * N + (q + 1) * QUAD)
                        load_bc(b + 1, q, "c")
                    for e in range(2):
                        sp.wait_ge(e_done, (b + 1) * GROUPS - (1 - e) * TT)
                        if is_first(b):
                            sp.wait_ge(w_kept[e], E // 2 * 16)
                        load_w(e)

            def more_input(b):
                if not (isinstance(b, int) and b == B - 2):
                    sp.wait_ge(proj_done, step_no(b, "NT3") + 1)
                    load_x(b + 2)
                send_bc(b + 1, step_no(b, "NS"))

            over_batches(sp, batch)
            for tt in range(2):
                load_xo(B - 1, tt)
            for tt in range(2):
                store(B - 1, tt)
                load_xo(B - 1, tt + 2)
            for tt in range(2, TT):
                store(B - 1, tt)
            for tt in range(2):
                sp.wait_ge(out_st[tt], B * 2 * 16)

        @block.gpsimd
        def _(pool):
            nc.gpsimd.memset(ident[:], 0.0).then_inc(const_p, 1)
            nc.gpsimd.memset(pick_f[:], 0.0).then_inc(const_p, 1)
            for e in range(E):
                nc.gpsimd.memset(iota[:, e:e + 1], float(e)).then_inc(const_p, 1)
            pool.wait_ge(const_p, 2 + E)
            nc.gpsimd.affine_select(out=ident[:], in_=ident[:], compare_op=ALU.not_equal, fill=1.0,
                                    base=0, pattern=[[-1, P]], channel_multiplier=1).then_inc(const_p, 1)
            for half_no in range(2):
                pool.wait_ge(const_p, 3 + E + half_no)
                nc.gpsimd.affine_select(out=pick_f[:], in_=pick_f[:], compare_op=ALU.not_equal, fill=1.0,
                                        base=-32 * half_no, pattern=[[-1, E]],
                                        channel_multiplier=1).then_inc(const_p, 1)

            def dbx_quad(b, j):
                dt, q = j // NQ, j % NQ
                if q == 0:
                    pool.wait_ge(u_ready, b * DT + dt + 1)
                if dt == 0:
                    pool.wait_ge(b_in[q], (b + 1) * 16)
                pool.wait_ge(scanned, from_start((b * DT * NQ + j - 1) * QUAD))
                nc.gpsimd.tensor_tensor(dbx[:, j % 2], b_sb[:, q * QUAD:(q + 1) * QUAD, :],
                                        u_sb[:, dt % 2, :].unsqueeze(1).to_broadcast([P, QUAD, T]),
                                        ALU.mult).then_inc(dbx_ready, 1)

            def gate_value(b, tt):
                if tt % 2 == 0:
                    pool.wait_ge(sig_ready, b * 2 + tt // 2 + 1)
                nc.gpsimd.tensor_tensor(acc[:, tt], acc[:, tt], sig[:, tt % 2], ALU.mult).then_inc(g_ready, 1)

            def add_x(b, tt):
                pool.wait_ge(sg_done, b * TT + tt + 1)
                pool.wait_ge(xo_in[tt % 2], (b * 2 + tt // 2 + 1) * 16)
                nc.gpsimd.tensor_tensor(xo[:, tt % 2], xo[:, tt % 2], s_sb[:, tt], ALU.add).then_inc(out_sum, 1)

            def batch(b, par):
                for j in range(DT * NQ):
                    dbx_quad(b, j)
                    if not is_first(b):
                        if j in (G_AT, G_AT + 1):
                            gate_value(b - 1, 2 * (j - G_AT))
                            gate_value(b - 1, 2 * (j - G_AT) + 1)
                        if G_AT + 2 <= j < G_AT + 2 + TT:
                            add_x(b - 1, j - G_AT - 2)

            over_batches(pool, batch)
            for tt in range(TT):
                gate_value(B - 1, tt)
            for tt in range(TT):
                add_x(B - 1, tt)

        @block.scalar
        def _(act):
            def ln_root(b):
                act.wait_ge(bn_done, b * 8 + 3)
                nc.scalar.activation(rstd[:], vpe[:], ACT.Ln).then_inc(ln_act, 1)
                act.wait_ge(ln_act, b * 2 + 1)
                nc.scalar.activation(rstd[:], rstd[:], ACT.Exp, scale=-0.5).then_inc(ln_act, 1)

            def copy_t(b, dt, no):
                act.wait_ge(proj_done, no + 1)
                if dt == 0:
                    act.wait_ge(u_ready, b * DT)
                    act.wait_ge(xd_ready, b * DT)
                    act.wait_ge(xl_ready, b * DT)
                nc.scalar.activation(xT[:, dt, :], proj_ps[:], ACT.Copy).then_inc(proj_used, 1)

            def split_x(b, dt):
                act.wait_ge(proj_used, t_copied(b, dt))
                act.wait_ge(e_done, b * GROUPS)
                act.wait_ge(xl_ready, from_start((b - 1) * DT + dt + 1))
                nc.scalar.activation(xh[:, dt, :], xT[:, dt, :], ACT.Copy).then_inc(xh_ready, 1)

            def copy_tok(b, pair, no):
                act.wait_ge(proj_done, no + 1)
                act.wait_ge(half_ready, b)
                nc.scalar.activation(tok[:, 2 * pair:2 * pair + 2, :],
                                     proj_ps[:, 0:2 * PROJ].rearrange("p (t r) -> p t r", r=PROJ),
                                     ACT.Copy).then_inc(proj_used, 1)

            def copy_dun(no):
                act.wait_ge(proj_done, no + 1)
                nc.scalar.activation(dun[:], proj_ps[:], ACT.Copy).then_inc(proj_used, 1)

            def copy_bc(b, no):
                act.wait_ge(proj_done, no + 1)
                act.wait_ge(bc_out, b * 16)
                nc.scalar.activation(bc_row[:], proj_ps[0:2 * N, :], ACT.Copy).then_inc(proj_used, 1)

            def softplus(b, dt, no):
                k = b * DT + dt
                act.wait_ge(proj_done, no + 1)
                act.wait_ge(da_ready, from_start((k - 1) * N))
                act.wait_ge(dbx_ready, from_start((k - 1) * NQ))
                bias = db_sb[:, dt:dt + 1]
                exp_part, max_part = u_sb[:, dt % 2, :], delta[:, dt % 2, :]
                nc.scalar.activation(exp_part, proj_ps[:], ACT.Abs, bias=bias).then_inc(sp_step, 1)
                nc.scalar.activation(max_part, proj_ps[:], ACT.Relu, bias=bias).then_inc(proj_used, 1)
                act.wait_ge(sp_step, k * 2 + 1)
                nc.scalar.activation(exp_part, exp_part, ACT.Exp, scale=-1.0).then_inc(sp_step, 1)
                act.wait_ge(sp_step, k * 2 + 2)
                nc.scalar.activation(exp_part, exp_part, ACT.Ln, bias=1.0).then_inc(sp_ready, 1)

            def times_d(b, dt):
                act.wait_ge(proj_used, t_copied(b, dt))
                act.wait_ge(xd_used, b * DT + dt)
                nc.scalar.activation(xD[:], xT[:, dt, :], ACT.Copy,
                                     scale=dpar_sb[:, dt:dt + 1]).then_inc(xd_ready, 1)

            def da_unit(b, par, j):
                dt, n = j // N, j % N
                u = b * UNITS + j
                if n == 0:
                    act.wait_ge(delta_ready, b * DT + dt + 1)
                act.wait_ge(p_ready, from_start(u - back(j, DA_BANKS) + 1))
                nc.scalar.activation(scan_ps[:, j % DA_BANKS, :], delta[:, dt % 2, :], ACT.Exp,
                                     scale=a_sb[:, dt, n:n + 1]).then_inc(da_ready, 1)

            def copy_y(b, dt):
                k = b * DT + dt
                act.wait_ge(p_used, (k + 1) * N)
                act.wait_ge(out_sum, b * TT)
                nc.scalar.activation(s_sb[:, :, dt * P:(dt + 1) * P], y_ps[:, dt % 2], ACT.Copy).then_inc(y_used, 1)

            def expert_relu(b, par, g):
                e, tt = g // TT, g % TT
                G = b * GROUPS + g
                act.wait_ge(e_done, G + 1)
                if g == 0:
                    act.wait_ge(half_ready, b + 1)
                if e == 0:
                    act.wait_ge(sg_done, from_start((b - 1) * TT + tt + 1))
                    dst = acc[:, tt]
                else:
                    a = b * ADDS + g - TT
                    act.wait_ge(e_added, from_start(a - 1))
                    act.wait_ge(g_ready, b * TT)
                    dst = relu[:, g % 2]
                nc.scalar.activation(dst, exp_ps[:, g % 2], ACT.Relu,
                                     scale=half[:, par, tt, e:e + 1]).then_inc(e_used, 1)

            def sigmoid(b, pair, part):
                c = (b * 2 + pair) * 2
                src = acc[:, 2 * pair:2 * pair + 2]
                if part == 0:
                    act.wait_ge(e_added, (b + 1) * ADDS)
                    act.wait_ge(g_ready, b * TT + 2 * pair)
                    nc.scalar.activation(sig[:], src, ACT.Exp, scale=-1.0).then_inc(sig_step, 1)
                if part == 1:
                    act.wait_ge(sig_step, c + 1)
                    nc.scalar.activation(sig[:], sig[:], ACT.Ln, bias=1.0).then_inc(sig_step, 1)
                if part == 2:
                    act.wait_ge(sig_step, c + 2)
                    nc.scalar.activation(sig[:], sig[:], ACT.Exp, scale=-1.0).then_inc(sig_ready, 1)

            act.add_instruction(mybir.InstLoadActFuncSet(
                name=nc.get_next_instruction_name(), act_func_set_id=6,
                engine=mybir.EngineType.Activation))
            ln_root(0)
            act.wait_ge(w_const, 9 * 16)
            nc.scalar.activation(a_sb[:], a_sb[:], ACT.Exp).then_inc(a_exp, 1)
            for dt in range(DT):
                copy_t(0, dt, step_no(None, f"NT{dt}"))
            for pair in range(2):
                copy_tok(0, pair, step_no(None, f"NX{pair}"))
            copy_dun(step_no(None, "NR"))
            copy_bc(0, step_no(None, "NS"))
            softplus(0, 0, step_no(None, "NZ0"))
            act.wait_ge(a_ready, 1)

            def batch(b, par):
                nxt = not is_last(b)
                for j in range(UNITS):
                    if j == 20 and nxt:
                        ln_root(b + 1)
                    name = STEPS.get(j - ACT_LAG + 1)
                    if name and (nxt or name[0] != "N"):
                        no = step_no(b, name)
                        if name[:2] == "NT":
                            copy_t(b + 1, int(name[2]), no)
                        elif name[:2] == "NX":
                            copy_tok(b + 1, int(name[2]), no)
                        elif name == "NR":
                            copy_dun(no)
                        elif name == "NS":
                            copy_bc(b + 1, no)
                        elif name == "NZ0":
                            softplus(b + 1, 0, no)
                        elif name[0] == "Z":
                            softplus(b, int(name[1]), no)
                    if j == 0:
                        times_d(b, 0)
                    if j % N == XD_AT and j // N < DT - 1:
                        times_d(b, j // N + 1)
                    if j - ACT_LAG in GROUP_AT:
                        expert_relu(b, par, GROUP_AT[j - ACT_LAG])
                    if j - ACT_LAG + UNITS in GROUP_AT and not is_first(b):
                        expert_relu(b - 1, 1 - par, GROUP_AT[j - ACT_LAG + UNITS])
                    if j == 2:
                        for dt in range(DT):
                            split_x(b, dt)
                    if j == Y_AT and not is_first(b):
                        copy_y(b - 1, DT - 1)
                    if j % N == 12 and j >= N:
                        copy_y(b, j // N - 1)
                    if not is_first(b) and SIG_AT <= j < SIG_AT + 6:
                        sigmoid(b - 1, (j - SIG_AT) // 3, (j - SIG_AT) % 3)
                    da_unit(b, par, j)

            over_batches(act, batch)
            for j in range(ACT_LAG):
                if j - ACT_LAG + UNITS in GROUP_AT:
                    expert_relu(B - 1, 1, GROUP_AT[j - ACT_LAG + UNITS])
            copy_y(B - 1, DT - 1)
            for pair in range(2):
                for part in range(3):
                    sigmoid(B - 1, pair, part)

        @block.vector
        def _(dve):
            def ln_stats(b, tt):
                dve.wait_ge(x_in, (b + 1) * 16)
                nc.vector.bn_stats(stats[:, tt, :], xn[:, tt, :]).then_inc(bn_done if tt == TT - 1 else bn_part, 1)

            def ln_var(b):
                dve.wait_ge(bn_part, (b + 1) * (TT - 1))
                dve.wait_ge(bn_done, b * 8 + 1)
                nc.vector.memset(pad[:], 0.0)
                for tt in range(TT):
                    last = nc.vector.bn_aggr(mv[:, tt, :], stats[:, tt, :])
                last.then_inc(bn_done, 1)
                dve.wait_ge(bn_done, b * 8 + 2)
                nc.vector.tensor_scalar(vpe[:], mv[:, :, 1], LN_EPS, None, ALU.add).then_inc(bn_done, 1)

            def ln_newton(b):
                dve.wait_ge(ln_act, b * 2 + 2)
                c = b * 8 + 3
                nc.vector.tensor_tensor(newt[:], rstd[:], rstd[:], ALU.mult).then_inc(bn_done, 1)
                dve.wait_ge(bn_done, c + 1)
                nc.vector.tensor_tensor(newt[:], newt[:], vpe[:], ALU.mult).then_inc(bn_done, 1)
                dve.wait_ge(bn_done, c + 2)
                nc.vector.tensor_scalar(newt[:], newt[:], -0.5, 1.5, ALU.mult, ALU.add).then_inc(bn_done, 1)
                dve.wait_ge(bn_done, c + 3)
                nc.vector.tensor_tensor(rstd[:], rstd[:], newt[:], ALU.mult).then_inc(bn_done, 1)
                dve.wait_ge(bn_done, c + 4)

            def ln_apply(b, tt):
                inst = nc.vector.tensor_scalar(xn[:, tt, :], xn[:, tt, :], mv[:, tt, 0:1], rstd[:, tt:tt + 1],
                                               ALU.subtract, ALU.mult)
                if tt == TT - 1:
                    inst.then_inc(bn_done, 1)
                else:
                    inst.then_inc(xn_ready, 1)

            def delta_u(b, dt):
                k = b * DT + dt
                dve.wait_ge(sp_ready, k + 1)
                dve.wait_ge(proj_used, t_copied(b, dt))
                dve.wait_ge(da_ready, from_start((k - 1) * N))
                nc.vector.tensor_tensor(delta[:, dt % 2, :], delta[:, dt % 2, :], u_sb[:, dt % 2, :],
                                        ALU.add).then_inc(delta_ready, 1)
                dve.wait_ge(delta_ready, k + 1)
                dve.wait_ge(dbx_ready, from_start((k - 1) * NQ))
                nc.vector.tensor_tensor(u_sb[:, dt % 2, :], delta[:, dt % 2, :], xT[:, dt, :],
                                        ALU.mult).then_inc(u_ready, 1)

            def split_x(b, dt):
                dve.wait_ge(xh_ready, b * DT + dt + 1)
                nc.vector.tensor_tensor(xl[:, dt, :], xT[:, dt, :], xh[:, dt, :].bitcast(F32),
                                        ALU.subtract).then_inc(xl_ready, 1)

            def split_w(e, c):
                dve.wait_ge(w_raw[c % 2], (e * (DT // 2) + c // 2 + 1) * 16)
                if c == 0:
                    dve.wait_ge(e_done, from_start((e - 1) * TT))
                    dve.wait_ge(w_kept[e % 2], e // 2 * 16)
                high = w_sb[:, e % 2, 0, c, :]
                nc.vector.tensor_copy(high, xo[:, c % 2]).then_inc(wh_done, 1)
                dve.wait_ge(wh_done, e * DT + c + 1)
                nc.vector.tensor_tensor(w_sb[:, e % 2, 1, c, :], xo[:, c % 2], high.bitcast(F32),
                                        ALU.subtract).then_inc(wl_done, 1)

            GATE_CHAIN = 5

            def gate(b, par, no):
                dve.wait_ge(proj_used, no + 1)
                c = b * GATE_CHAIN
                nc.vector.tensor_tensor(logit[:], tok[:, :, R + 2 * N:],
                                        gb_sb[:].unsqueeze(1).to_broadcast([P, TT, E]), ALU.add).then_inc(gate_step, 1)
                dve.wait_ge(gate_step, c + 1)
                nc.vector.memset(pad[:], 0.0)
                for tt in range(TT):
                    last = nc.vector.max(top[:, tt, :], logit[:, tt, :])
                last.then_inc(gate_step, 1)
                dve.wait_ge(gate_step, c + 2)
                nc.vector.memset(pad[:], 0.0)
                for tt in range(TT):
                    last = nc.vector.max_index(topi[:, tt, :], top[:, tt, :], logit[:, tt, :])
                last.then_inc(gate_step, 1)
                dve.wait_ge(gate_step, c + 3)
                nc.vector.tensor_copy(topf[:], topi[:]).then_inc(gate_step, 1)
                dve.wait_ge(gate_step, c + 4)
                for tt in range(TT):
                    for s in range(2):
                        last = nc.vector.tensor_scalar(hot[:, s, tt, :], iota[:], topf[:, tt, s:s + 1], 0.5,
                                                       ALU.is_equal, ALU.mult)
                last.then_inc(gate_step, 1)
                dve.wait_ge(gate_step, c + 5)
                dve.wait_ge(e_used, from_start((b - 1) * GROUPS))
                nc.vector.tensor_tensor(half[:, par], hot[:, 0], hot[:, 1], ALU.add).then_inc(half_ready, 1)

            def scan(b, j):
                u = b * UNITS + j
                dve.wait_ge(da_ready, u + 1)
                if j % QUAD == 0:
                    dve.wait_ge(dbx_ready, b * DT * NQ + j // QUAD + 1)
                bank = scan_ps[:, j % DA_BANKS, :]
                nc.vector.tensor_tensor_scan(bank, bank, dbx[:, (j // QUAD) % 2, j % QUAD, :], 0.0,
                                             ALU.mult, ALU.add).then_inc(scanned, 1)

            def times_c(b, j):
                dt, n = j // N, j % N
                u = b * UNITS + j
                dve.wait_ge(scanned, u + 1)
                if dt == 0 and n % QUAD == 0:
                    dve.wait_ge(c_in[n // QUAD], (b + 1) * 16)
                dve.wait_ge(p_used, from_start(u - back(j, P_SLOTS) + 1))
                nc.vector.tensor_tensor(p_sb[:, j % P_SLOTS, :], scan_ps[:, j % DA_BANKS, :], c_sb[:, n, :],
                                        ALU.mult).then_inc(p_ready, 1)

            def expert_add(b, g):
                tt = g % TT
                a = b * ADDS + g - TT
                dve.wait_ge(e_used, b * GROUPS + g + 1)
                dve.wait_ge(e_added, from_start(a - TT + 1))
                nc.vector.tensor_tensor(acc[:, tt], acc[:, tt], relu[:, g % 2], ALU.add).then_inc(e_added, 1)

            def times_g(b, tt):
                dve.wait_ge(y_used, (b + 1) * DT)
                dve.wait_ge(g_ready, b * TT + tt + 1)
                nc.vector.tensor_tensor(s_sb[:, tt], s_sb[:, tt], acc[:, tt], ALU.mult).then_inc(sg_done, 1)

            for tt in range(TT):
                ln_stats(0, tt)
            ln_var(0)
            ln_newton(0)
            for tt in range(TT):
                ln_apply(0, tt)
            dve.wait_ge(a_exp, 1)
            nc.vector.tensor_scalar(a_sb[:], a_sb[:], -1.0, None, ALU.mult).then_inc(a_ready, 1)
            dve.wait_ge(const_p, 5 + E)
            nc.vector.tensor_copy(pick[:], pick_f[:]).then_inc(eb_step, 1)
            nc.vector.memset(eb_sb[:].bitcast(F32), 0.0).then_inc(eb_step, 1)
            dve.wait_ge(eb_step, 2)
            dve.wait_ge(w_const, 9 * 16)
            for lo in (0, 32):
                nc.vector.tensor_copy(eb_sb[lo:lo + E, :], s_sb[lo:lo + E, 0, :]).then_inc(eb_step, 1)
            dve.wait_ge(eb_step, 4)
            nc.vector.tensor_tensor(eb_sb[32:32 + E, :], s_sb[32:32 + E, 0, :], eb_sb[32:32 + E, :].bitcast(F32),
                                    ALU.subtract).then_inc(eb_step, 1)
            gate(0, 0, step_no(None, "NX1"))
            delta_u(0, 0)

            def batch(b, par):
                nxt = not is_last(b)
                for j in range(UNITS):
                    scan(b, j)
                    if nxt:
                        if j in (15, 16):
                            ln_stats(b + 1, 2 * (j - 15))
                            ln_stats(b + 1, 2 * (j - 15) + 1)
                        if j == 17:
                            ln_var(b + 1)
                        if j == 21:
                            ln_newton(b + 1)
                        if j in (22, 24):
                            ln_apply(b + 1, j - 22)
                            ln_apply(b + 1, j - 21)
                    if j in (1, 2, 3, 4):
                        split_x(b, j - 1)
                    if is_first(b):
                        if j == 5:
                            for c in range(DT):
                                split_w(0, c)
                        if j >= 10 and (j - 3) % 7 < DT and (j - 3) // 7 < E:
                            split_w((j - 3) // 7, (j - 3) % 7)
                    name = STEPS.get(j - GATE_LAG)
                    if name == "NX1" and nxt:
                        gate(b + 1, 1 - par, step_no(b, name))
                    name = STEPS.get(j - DVE_LAG)
                    if name and name[0] == "Z":
                        delta_u(b, int(name[1]))
                    if name == "NZ0" and nxt:
                        delta_u(b + 1, 0)
                    if j - DVE_LAG + UNITS in GROUP_AT and not is_first(b):
                        expert_add(b - 1, GROUP_AT[j - DVE_LAG + UNITS])
                    if j - DVE_LAG in GROUP_AT and GROUP_AT[j - DVE_LAG] >= TT:
                        expert_add(b, GROUP_AT[j - DVE_LAG])
                    if not is_first(b) and j in TIMES_G_AT:
                        times_g(b - 1, TIMES_G_AT.index(j))
                    if j >= 1:
                        times_c(b, j - 1)
                times_c(b, UNITS - 1)

            over_batches(dve, batch)
            for j in range(DVE_LAG):
                if j - DVE_LAG + UNITS in GROUP_AT:
                    expert_add(B - 1, GROUP_AT[j - DVE_LAG + UNITS])
            for tt in range(TT):
                times_g(B - 1, tt)

        @block.tensor
        def _(pe):
            def bank_free(no):
                pe.wait_ge(proj_used, no)

            def turn_x(b, dt, no):
                bank_free(no)
                if dt == 0:
                    pe.wait_ge(bn_done, (b + 1) * 8)
                    pe.wait_ge(xn_ready, (b + 1) * (TT - 1))
                for tt in range(TT):
                    last = nc.tensor.matmul(proj_ps[:, tt * P:(tt + 1) * P], xn[:, tt, dt * P:(dt + 1) * P],
                                            ident[:], start=True, stop=True, is_transpose=True)
                last.then_inc(proj_done, 1)

            def x_proj_gate(pair, no):
                bank_free(no)
                for tt in (2 * pair, 2 * pair + 1):
                    for c in range(DT):
                        last = nc.tensor.matmul(proj_ps[:, (tt % 2) * PROJ:(tt % 2 + 1) * PROJ],
                                                xT[:, c, tt * P:(tt + 1) * P], xwg_sb[:, c, :],
                                                start=(c == 0), stop=(c == DT - 1))
                last.then_inc(proj_done, 1)

            def turn_tok(lo, hi, no):
                bank_free(no)
                for tt in range(TT):
                    last = nc.tensor.matmul(proj_ps[0:hi - lo, tt * P:(tt + 1) * P], tok[:, tt, lo:hi],
                                            ident[:], start=True, stop=True, is_transpose=True)
                last.then_inc(proj_done, 1)

            def dt_proj(dt, no):
                bank_free(no)
                nc.tensor.matmul(proj_ps[:], dw_sb[:, dt * P:(dt + 1) * P], dun[:],
                                 start=True, stop=True).then_inc(proj_done, 1)

            def expert(b, g):
                e, tt = g // TT, g % TT
                if g == 0:
                    pe.wait_ge(xl_ready, (b + 1) * DT)
                if tt == 0 and is_first(b):
                    pe.wait_ge(wl_done, (e + 1) * DT)
                elif tt == 0:
                    pe.wait_ge(w_in[e % 2], ((b - 1) * (E // 2) + e // 2 + 1) * 16)
                pe.wait_ge(e_used, from_start(b * GROUPS + g - 1))
                dst = exp_ps[:, g % 2]
                w_high, w_low = w_sb[:, e % 2, 0], w_sb[:, e % 2, 1]
                for c in range(DT):
                    high, low = xh[:, c, tt * P:(tt + 1) * P], xl[:, c, tt * P:(tt + 1) * P]
                    nc.tensor.matmul(dst, high, w_high[:, c, :], start=(c == 0), stop=False)
                    nc.tensor.matmul(dst, high, w_low[:, c, :], start=False, stop=False)
                    nc.tensor.matmul(dst, low, w_high[:, c, :], start=False, stop=False)
                nc.tensor.matmul(dst, pick[:, e:e + 1].to_broadcast([EB_ROWS, P]), eb_sb[:],
                                 start=False, stop=True).then_inc(e_done, 1)

            def add_y(b, j):
                dt, n = j // N, j % N
                k = b * DT + dt
                y = y_ps[:, dt % 2]
                if n == 0:
                    pe.wait_ge(y_used, from_start(k - 1))
                pe.wait_ge(p_ready, b * UNITS + j + 1)
                for tt in range(TT):
                    last = nc.tensor.matmul(y[:, tt, :], p_sb[:, j % P_SLOTS, tt * P:(tt + 1) * P], ident[:],
                                            start=(n == 0 and tt == 0), stop=(n == N - 1), is_transpose=True,
                                            skip_group_check=True)
                last.then_inc(p_used, 1)
                if n == XD_ADD_AT:
                    pe.wait_ge(xd_ready, k + 1)
                    for tt in range(TT):
                        last = nc.tensor.matmul(y[:, tt, :], xD[:, tt * P:(tt + 1) * P], ident[:],
                                                start=False, stop=False, is_transpose=True,
                                                skip_group_check=True)
                    last.then_inc(xd_used, 1)

            def steps_for(name, b, no):
                if name[:2] == "NT":
                    turn_x(b, int(name[2]), no)
                elif name[:2] == "NX":
                    x_proj_gate(int(name[2]), no)
                elif name == "NR":
                    turn_tok(0, R, no)
                elif name == "NS":
                    turn_tok(R, R + 2 * N, no)
                elif name == "NZ0":
                    dt_proj(0, no)

            pe.wait_ge(const_p, 5 + E)
            pe.wait_ge(eb_step, 5)
            for name in LEAD_STEPS:
                if name == "NX0":
                    pe.wait_ge(w_const, 9 * 16)
                steps_for(name, 0, step_no(None, name))

            def batch(b, par):
                for j in range(UNITS):
                    name = STEPS.get(j)
                    if name and name[0] == "N":
                        if not is_last(b):
                            steps_for(name, b + 1, step_no(b, name))
                    elif name:
                        dt_proj(int(name[1]), step_no(b, name))
                    if j in GROUP_AT:
                        expert(b, GROUP_AT[j])
                    add_y(b, j)

            over_batches(pe, batch)


_SHAPES = {"out": (16, 512, 512)}


def kernel(L0_attn_x, L0_attn_x_proj_w, L0_attn_dt_proj_w, L0_attn_dt_proj_b, L0_attn_A_log, L0_attn_D_param,
           L0_ffn_gate_w, L0_ffn_gate_b, L0_ffn_expert_w, L0_ffn_expert_b):
    import numpy as np
    import concourse.bacc as bacc
    from concourse import mybir as mb
    from concourse.bass_utils import run_bass_kernel_spmd

    def lay(a):
        return np.ascontiguousarray(a)

    def by_tile(a):
        a = np.asarray(a)
        return lay(np.moveaxis(a.reshape(a.shape[0] // 128, 128, *a.shape[1:]), 0, 1))

    arrays = {
        "x": lay(L0_attn_x),
        "xw": lay(np.asarray(L0_attn_x_proj_w).T),
        "dw": lay(np.asarray(L0_attn_dt_proj_w).T),
        "db": by_tile(L0_attn_dt_proj_b),
        "alog": by_tile(L0_attn_A_log),
        "dpar": by_tile(L0_attn_D_param),
        "gw": lay(L0_ffn_gate_w),
        "gb": lay(np.asarray(L0_ffn_gate_b).reshape(1, -1)),
        "ew": lay(L0_ffn_expert_w),
        "eb": lay(L0_ffn_expert_b),
    }
    nc = bacc.Bacc("TRN2", target_bir_lowering=False, num_devices=1)
    args = [nc.dram_tensor(f"in_{n}", a.shape, mb.dt.from_np(a.dtype), kind="ExternalInput").ap()
            for n, a in arrays.items()]
    out = nc.dram_tensor("out", _SHAPES["out"], mb.dt.float32, kind="ExternalOutput").ap()
    build(nc, *args, out)
    r = run_bass_kernel_spmd(nc, [{f"in_{n}": a for n, a in arrays.items()}], core_ids=[0])
    return r.results[0]["out"]
```
